# Optimizing a Trainium2 kernel written in Bass

```python
import numpy as np
import jax
import jax.numpy as jnp

def _softmax(x, axis=-1):
    return jax.nn.softmax(x, axis=axis)

def _gelu(x):
    return jax.nn.gelu(x, approximate=True)

def _silu(x):
    return jax.nn.silu(x)

def _sigmoid(x):
    return jax.nn.sigmoid(x)

def _layernorm(x, axis=-1, eps=1e-05):
    m = jnp.mean(x, axis=axis, keepdims=True)
    v = jnp.var(x, axis=axis, keepdims=True)
    return (x - m) / jnp.sqrt(v + eps)

def _scatter_add(tgt, idx, src, axis=0):
    return tgt.at[idx].add(src)

def _segment_sum(src, seg, n):
    return jax.ops.segment_sum(src, seg, n)
kernel_name = 'mk_seq_preln_d1_jaxref_r8_e99c20'

def setup_inputs(seed: int=0):
    np.random.seed(seed)
    _w = jnp.asarray

    def _L0_attn_setup():
        import jax, jax.numpy as jnp
        import numpy as np
        B, S, H = (1, 256, 512)
        NH = 32
        Q_LORA, KV_LORA = (192, 64)
        QK_NOPE, QK_ROPE = (128, 64)
        Q_HEAD = QK_NOPE + QK_ROPE
        V_HEAD = 128
        key = jax.random.key(seed)
        ks = jax.random.split(key, 12)

        def lin(k, out_d, in_d):
            s = 1.0 / np.sqrt(in_d)
            return jax.random.uniform(k, (out_d, in_d), jnp.float32, -s, s)
        return {'hidden_size': jax.random.normal(ks[0], (B, S, H), jnp.float32), 'Wq_c': lin(ks[1], Q_LORA, H), 'bq_c': jnp.zeros((Q_LORA,), jnp.float32), 'Wq_up': lin(ks[2], NH * Q_HEAD, Q_LORA), 'bq_up': jnp.zeros((NH * Q_HEAD,), jnp.float32), 'Wkv_c': lin(ks[3], KV_LORA + QK_ROPE, H), 'bkv_c': jnp.zeros((KV_LORA + QK_ROPE,), jnp.float32), 'Wkv_up': lin(ks[4], NH * (QK_NOPE + V_HEAD), KV_LORA), 'bkv_up': jnp.zeros((NH * (QK_NOPE + V_HEAD),), jnp.float32), 'Wo': lin(ks[5], H, V_HEAD), 'bo': jnp.zeros((H,), jnp.float32)}
    _L0_attn_in = _L0_attn_setup()

    def _L0_ffn_setup():
        import jax, jax.numpy as jnp
        import numpy as np
        import math
        D = 512
        TOKENS = (4, 256)
        P = 0.8

        def conn_dense(kernel, x):
            w = jnp.where(kernel, jnp.asarray(1.0, x.dtype), jnp.asarray(-1.0, x.dtype))
            return x @ w

        def ei_dense(x, kernel, scale, p):
            in_dim = x.shape[-1]
            ne = round(in_dim * p)
            x_exc = x[..., :ne]
            x_inh = x[..., ne:]
            xx = jnp.concatenate([x_exc, -p / (1.0 - p) * x_inh], axis=-1)
            return scale * conn_dense(kernel, xx)
        key = jax.random.key(seed)
        ks = jax.random.split(key, 4)
        x = jax.random.normal(ks[0], (*TOKENS, D), dtype=jnp.float32)
        k0 = jax.random.bernoulli(ks[1], 0.5, (D, D))
        k1 = jax.random.bernoulli(ks[2], 0.5, (D, D))
        k2 = jax.random.bernoulli(ks[3], 0.5, (D, D))
        s = jnp.asarray(1.0 / math.sqrt(D), dtype=jnp.float32)
        return {'x': x, 'k0': k0, 's0': s, 'k1': k1, 's1': s, 'k2': k2, 's2': s}
    _L0_ffn_in = _L0_ffn_setup()
    _d = {'L0_attn_hidden_size': _L0_attn_in['hidden_size'], 'L0_attn_Wq_c': _L0_attn_in['Wq_c'], 'L0_attn_bq_c': _L0_attn_in['bq_c'], 'L0_attn_Wq_up': _L0_attn_in['Wq_up'], 'L0_attn_bq_up': _L0_attn_in['bq_up'], 'L0_attn_Wkv_c': _L0_attn_in['Wkv_c'], 'L0_attn_bkv_c': _L0_attn_in['bkv_c'], 'L0_attn_Wkv_up': _L0_attn_in['Wkv_up'], 'L0_attn_bkv_up': _L0_attn_in['bkv_up'], 'L0_attn_Wo': _L0_attn_in['Wo'], 'L0_attn_bo': _L0_attn_in['bo'], 'L0_ffn_k0': _L0_ffn_in['k0'], 'L0_ffn_s0': _L0_ffn_in['s0'], 'L0_ffn_k1': _L0_ffn_in['k1'], 'L0_ffn_s1': _L0_ffn_in['s1'], 'L0_ffn_k2': _L0_ffn_in['k2'], 'L0_ffn_s2': _L0_ffn_in['s2']}
    _x0 = _d['L0_attn_hidden_size']
    _d['L0_attn_hidden_size'] = jax.random.normal(jax.random.fold_in(jax.random.key(seed), 1), (2, 1024, 512), dtype=_x0.dtype)
    del _x0
    return _d

def reference(L0_attn_hidden_size, L0_attn_Wq_c, L0_attn_bq_c, L0_attn_Wq_up, L0_attn_bq_up, L0_attn_Wkv_c, L0_attn_bkv_c, L0_attn_Wkv_up, L0_attn_bkv_up, L0_attn_Wo, L0_attn_bo, L0_ffn_k0, L0_ffn_s0, L0_ffn_k1, L0_ffn_s1, L0_ffn_k2, L0_ffn_s2):

    def _L0_attn_ref(hidden_size, Wq_c, bq_c, Wq_up, bq_up, Wkv_c, bkv_c, Wkv_up, bkv_up, Wo, bo):
        import jax, jax.numpy as jnp
        import numpy as np
        B, S, H = (1, 256, 512)
        NH = 32
        Q_LORA, KV_LORA = (192, 64)
        QK_NOPE, QK_ROPE = (128, 64)
        Q_HEAD = QK_NOPE + QK_ROPE
        V_HEAD = 128
        b, s, _ = hidden_size.shape
        q_c = hidden_size @ Wq_c.T + bq_c
        q = (q_c @ Wq_up.T + bq_up).reshape(b, s, NH, Q_HEAD).transpose(0, 2, 1, 3)
        kv = hidden_size @ Wkv_c.T + bkv_c
        kv_nope, kv_rope = (kv[..., :KV_LORA], kv[..., KV_LORA:])
        kvu = (kv_nope @ Wkv_up.T + bkv_up).reshape(b, s, NH, QK_NOPE + V_HEAD).transpose(0, 2, 1, 3)
        k_nope, v = (kvu[..., :QK_NOPE], kvu[..., QK_NOPE:])
        k_rope = jnp.broadcast_to(kv_rope[:, None, :, :], (b, NH, s, QK_ROPE))
        k = jnp.concatenate([k_nope, k_rope], axis=-1)
        scores = jnp.einsum('bhqd,bhkd->bhqk', q, k) / np.sqrt(Q_HEAD)
        attn = jax.nn.softmax(scores, axis=-1)
        o = jnp.einsum('bhqk,bhkv->bhqv', attn, v)
        out = jnp.einsum('bhsv,Hv->bsH', o, Wo) + bo
        return out

    def _L0_ffn_ref(x, k0, s0, k1, s1, k2, s2):
        import jax, jax.numpy as jnp
        import numpy as np
        import math
        D = 512
        TOKENS = (4, 256)
        P = 0.8

        def conn_dense(kernel, x):
            w = jnp.where(kernel, jnp.asarray(1.0, x.dtype), jnp.asarray(-1.0, x.dtype))
            return x @ w

        def ei_dense(x, kernel, scale, p):
            in_dim = x.shape[-1]
            ne = round(in_dim * p)
            x_exc = x[..., :ne]
            x_inh = x[..., ne:]
            xx = jnp.concatenate([x_exc, -p / (1.0 - p) * x_inh], axis=-1)
            return scale * conn_dense(kernel, xx)
        h = s0 * conn_dense(k0, x)
        h = jax.nn.relu(h) * 2.0
        h = ei_dense(h, k1, s1, P)
        h = jax.nn.relu(h) * 2.0
        return ei_dense(h, k2, s2, P)
    x = L0_attn_hidden_size
    x = x + _L0_attn_ref(_layernorm(x, axis=-1), L0_attn_Wq_c, L0_attn_bq_c, L0_attn_Wq_up, L0_attn_bq_up, L0_attn_Wkv_c, L0_attn_bkv_c, L0_attn_Wkv_up, L0_attn_bkv_up, L0_attn_Wo, L0_attn_bo)
    x = x + _L0_ffn_ref(_layernorm(x, axis=-1), L0_ffn_k0, L0_ffn_s0, L0_ffn_k1, L0_ffn_s1, L0_ffn_k2, L0_ffn_s2)
    return x

_drawn_inputs = setup_inputs


def setup_inputs(seed=0):
    import zlib

    import numpy as np

    out = dict(_drawn_inputs(seed))
    spreads = {'L0_attn_bq_c': (0.0, 0.8),
     'L0_attn_bq_up': (0.0, 0.8),
     'L0_attn_bkv_c': (0.0, 0.1),
     'L0_attn_bkv_up': (0.0, 0.1),
     'L0_attn_bo': (0.0, 0.1)}
    factors = {'L0_attn_Wq_c': 3.935, 'L0_attn_Wq_up': 3.698}
    for name, (base, spread) in spreads.items():
        noise = np.random.default_rng([zlib.crc32(name.encode()), seed]).standard_normal(out[name].shape)
        drawn = base * np.exp(spread * noise) if base else spread * noise
        out[name] = jnp.asarray(drawn.astype(out[name].dtype))
    for name, factor in factors.items():
        out[name] = (out[name] * factor).astype(out[name].dtype)
    return out
```

```python
from contextlib import ExitStack

import numpy as np
import concourse.bass as bass
from concourse import mybir

F32 = mybir.dt.float32
F32R = mybir.dt.float32r
U8 = mybir.dt.uint8
ACT = mybir.ActivationFunctionType
ALU = mybir.AluOpType
AX = mybir.AxisListType
ds = bass.ds

P = 128
NH = 32
NOPE, ROPE, VH = 128, 64, 128
QHEAD = NOPE + ROPE
QL, KVL = 192, 64
QB = QL - P
HID = 512
KT = HID // P
BATCH, SEQ = 2, 1024
TOK = BATCH * SEQ
TT = TOK // P
BLK = 512
NB = TOK // BLK
UN = BLK // P
KEYT = SEQ // P
NG = NB * NH
EPS = 1e-5
SCALE = float(1.0 / np.sqrt(QHEAD))
EXC = round(HID * 0.8)
INH = float(np.float32(-0.8 / (1.0 - 0.8)))
R_WK, R_BK, R_BQ, R_QR, R_N = 256, 320, 321, 322, 450
HG = 4


def f32(ap):
    return ap.bitcast(F32)


def prepare(nc, dram, keep):
    with ExitStack() as ctx:
        sb = lambda n, s, d=F32: ctx.enter_context(nc.sbuf_tensor(n, s, d))
        ps = lambda n: ctx.enter_context(nc.psum_tensor(n, [P, 512], F32))
        sem = lambda n: ctx.enter_context(nc.semaphore(n))
        raw = [sb(f"raw{i}", [P, HG, R_N]) for i in range(2)]
        full = sb("w_full", [P, HG, 2, P])
        high = sb("w_high", [P, HG, 2, P], F32R)
        split = [sb(f"w_split{i}", [P, HG, 3, P], F32R) for i in range(2)]
        wcA, wcB, bqk = sb("wcA", [P, NH]), sb("wcB", [P, NH]), sb("bqk", [P, NH])
        bqr = sb("bqr", [P, NH])
        x_all = sb("x_all", [P, TT, HID])
        xn = [sb(f"xn{i}", [P, HID]) for i in range(2)]
        xnT = sb("xnT", [P, KT, TOK])
        wqc, wkvc = sb("wqc", [P, KT, 2 * P]), sb("wkvc", [P, KT, P])
        pb = sb("proj_bias", [P, 3])
        st, mv = sb("st", [P, TT, 6]), sb("mv", [P, TT, 2])
        std, rstd = sb("std", [P, TT]), sb("rstd", [P, TT])
        eps, ones = sb("eps", [P, 1]), sb("ones", [P, P])
        kvf, qaf, qbf = sb("kvf", [P, BLK]), sb("qaf", [P, BLK]), sb("qbf", [P, BLK])
        psA, psB, psC = ps("psA"), ps("psB"), ps("psC")
        psT = [ps("psT0"), ps("psT1")]
        psN, psD = ps("psN"), ps("psD")
        raw_in = [sem(f"raw_in{i}") for i in range(2)]
        split_out = [sem(f"split_out{i}") for i in range(2)]
        x_in = [sem(f"x_in{i}") for i in range(NB)]
        bias_in, w_in, absorbed, emptied, split_done, const = (
            sem(n) for n in ("bias_in", "w_in", "absorbed", "emptied", "split_done", "const"))
        step, std_done, xn_ready, xn_used, xnT_ready = (
            sem(n) for n in ("step", "std_done", "xn_ready", "xn_used", "xnT_ready"))
        proj_done, proj_out, c_done, n_done, c_out = (
            sem(n) for n in ("proj_done", "proj_out", "c_done", "n_done", "c_out"))
        groups = NH // HG
        W = 66
        vA = psA[:, 0:HG * W].rearrange("p (h c) -> p h c", c=W)
        vB = psB[:, 0:HG * W].rearrange("p (h c) -> p h c", c=W)
        vC = psC[:, 0:HG * 2].rearrange("p (h c) -> p h c", c=2)
        ident = keep["ident"]
        block = ctx.enter_context(nc.Block())

        @block.gpsimd
        def _(pool):
            for free in (emptied, xnT_ready, proj_out, c_out, split_done, xn_used, *split_out):
                pool.sem_inc(free, 1)
            nc.gpsimd.memset(ident[:], 0.0).then_inc(const, 1)
            nc.gpsimd.memset(ones[:], 1.0).then_inc(const, 1)
            nc.gpsimd.memset(eps[:], EPS).then_inc(const, 1)
            pool.wait_ge(const, 3)
            nc.gpsimd.affine_select(out=ident[:], in_=ident[:], compare_op=ALU.not_equal, fill=1.0, base=0,
                                    pattern=[[-1, P]], channel_multiplier=1).then_inc(const, 1)

        @block.sync
        def _(sp):
            def load(g, i):
                sp.dma_start(raw[i][:], dram["raw"][g].rearrange("p (h c) -> p h c", h=HG)).then_inc(raw_in[i], 16)

            def store(g, i):
                sp.dma_start(dram["weff"][g].rearrange("h p c -> p h c"),
                             f32(split[i][:].rearrange("p h t c -> p h (t c)"))).then_inc(split_out[i], 16)

            load(0, 0)
            load(1, 1)
            sp.dma_start(bqr[P - ROPE:P, :], dram["bqrT"]).then_inc(bias_in, 16)
            for n in range(NB):
                sp.dma_start(x_all[:, UN * n:UN * (n + 1), :],
                             dram["x"][n * BLK:(n + 1) * BLK, :].rearrange("(t p) d -> p t d", p=P)).then_inc(x_in[n], 16)
            sp.dma_start(wqc[:], dram["wqcT"].rearrange("(k p) c -> p k c", p=P)).then_inc(w_in, 16)
            sp.dma_start(wkvc[:], dram["wkvcT"].rearrange("(k p) c -> p k c", p=P)).then_inc(w_in, 16)
            sp.dma_start(pb[:], dram["pb"]).then_inc(w_in, 16)
            with sp.Fori(0, groups // 2 - 1) as g2:
                for i in range(2):
                    sp.wait_ge(split_done, 2 * g2 + i + 2)
                    store(2 * g2 + i, i)
                    load(2 * g2 + i + 2, i)
            for i in range(2):
                sp.wait_ge(split_done, groups + i)
                store(groups - 2 + i, i)
            for i in range(2):
                sp.wait_ge(split_out[i], 16 * (groups // 2) + 1)

        @block.tensor
        def _(pe):
            mm = nc.tensor.matmul
            with pe.Fori(0, groups // 2) as g2:
                for i in range(2):
                    pe.wait_ge(raw_in[i], 16 * (g2 + 1))
                    pe.wait_ge(emptied, 2 * g2 + i + 1)
                    for h in range(HG):
                        right = raw[i][:, h, R_WK:R_WK + W]
                        mm(vA[:, h, :], raw[i][:, h, 0:P], right, start=True, stop=True)
                        mm(vB[:, h, :], raw[i][:, h, P:2 * P], right, start=True, stop=True)
                        last = mm(vC[0:KVL, h, :], raw[i][:, h, R_WK:R_BK], raw[i][:, h, R_BK:R_QR],
                                  start=True, stop=True)
                    last.then_inc(absorbed, 1)
            pe.wait_ge(const, 4)
            with pe.Fori(0, TT // 2) as t2:
                for i in range(2):
                    if i == 0:
                        pe.wait_ge(xnT_ready, 2 * t2 + 1)
                    pe.wait_ge(xn_ready, 2 * t2 + i + 1)
                    for k in range(KT):
                        last = nc.tensor.transpose(psT[i][:, k * P:(k + 1) * P], xn[i][:, k * P:(k + 1) * P], ident[:])
                    last.then_inc(xn_used, 1)
            pe.wait_ge(xnT_ready, TT + 1)
            pe.wait_ge(w_in, 48)
            with pe.Fori(0, NB) as n:
                pe.wait_ge(proj_out, 3 * n + 1)
                for out, w, c in ((psA, wkvc, 0), (psB, wqc, 0), (psC, wqc, P)):
                    for k in range(KT):
                        last = mm(out[:], w[:, k, c:c + P], xnT[:, k, ds(n * BLK, BLK)], start=(k == 0), stop=(k == KT - 1))
                    last.then_inc(proj_done, 1)
                pe.wait_ge(proj_out, 3 * n + 4)
                pe.wait_ge(c_out, 2 * n + 1)
                for u in range(UN):
                    tok = slice(u * P, (u + 1) * P)
                    out = psD[:, u * NH:(u + 1) * NH]
                    mm(out, qaf[:, tok], wcA[:], start=True, stop=False)
                    mm(out, qbf[0:QB, tok], wcB[0:QB, :], start=False, stop=False)
                    last = mm(out, ones[:], bqk[:], start=False, stop=True)
                last.then_inc(c_done, 1)
                for u in range(UN):
                    tok = slice(u * P, (u + 1) * P)
                    last = nc.tensor.transpose(psN[:, u * KVL:(u + 1) * KVL], kvf[0:KVL, tok], ident[0:KVL, 0:KVL])
                last.then_inc(n_done, 1)

        @block.scalar
        def _(act):
            with act.Fori(0, groups // 2) as g2:
                for i in range(2):
                    act.wait_ge(absorbed, 2 * g2 + i + 1)
                    act.wait_ge(split_done, 2 * g2 + i + 1)
                    heads = ds((2 * g2 + i) * HG, HG)
                    nc.scalar.activation(full[:, :, 0, 0:KVL], vA[:, :, 0:KVL], ACT.Copy, scale=SCALE)
                    nc.scalar.activation(full[:, :, 1, 0:KVL], vB[:, :, 0:KVL], ACT.Copy, scale=SCALE)
                    nc.scalar.activation(wcA[:, heads], vA[:, :, KVL], ACT.Copy, scale=SCALE)
                    nc.scalar.activation(wcB[:, heads], vB[:, :, KVL], ACT.Copy, scale=SCALE)
                    nc.scalar.activation(keep["beff"][0:KVL, heads], vC[0:KVL, :, 1], ACT.Copy,
                                         scale=SCALE).then_inc(emptied, 1)
            act.wait_ge(step, TT * 2)
            act.wait_ge(const, 3)
            nc.scalar.activation(std[:], mv[:, :, 1], ACT.Sqrt, bias=eps[:]).then_inc(std_done, 1)
            with act.Fori(0, TT // 2) as t2:
                for i in range(2):
                    act.wait_ge(xn_used, 2 * t2 + i + 2)
                    nc.scalar.activation(xnT[:, :, ds((2 * t2 + i) * P, P)],
                                         psT[i][:].rearrange("p (k c) -> p k c", k=KT), ACT.Copy).then_inc(xnT_ready, 1)
            act.wait_ge(w_in, 48)
            with act.Fori(0, NB) as n:
                act.wait_ge(c_out, 2 * n + 1)
                for j, (out, src) in enumerate(((kvf, psA), (qaf, psB), (qbf, psC))):
                    act.wait_ge(proj_done, 3 * n + j + 1)
                    nc.scalar.activation(out[:], src[:], ACT.Identity, bias=pb[:, j:j + 1]).then_inc(proj_out, 1)

        @block.vector
        def _(dve):
            v = nc.vector
            done = sem("dve_done")
            count = [0]

            def link(ins):
                count[0] += 1
                ins.then_inc(done, 1)
                dve.wait_ge(done, count[0])

            dve.wait_ge(bias_in, 16)
            link(v.tensor_scalar(keep["beff"][KVL:P, :], bqr[KVL:P, :], SCALE, None, ALU.mult))
            per = 4
            with dve.Fori(0, groups // 2) as g2:
                for i in range(2):
                    g = 2 * g2 + i
                    base = 1 + per * g
                    dve.wait_ge(split_done, g + 1)
                    heads = ds(g * HG, HG)
                    dve.wait_ge(raw_in[i], 16 * (g2 + 1))
                    v.scalar_tensor_tensor(out=bqk[:, heads], in0=raw[i][:, :, R_BK], scalar=SCALE,
                                           in1=raw[i][:, :, R_BQ], op0=ALU.mult, op1=ALU.mult)
                    v.tensor_scalar(full[:, :, :, KVL:P], raw[i][:, :, R_QR:R_N].rearrange("p h (s c) -> p h s c", s=2),
                                    SCALE, None, ALU.mult).then_inc(done, 1)
                    dve.wait_ge(emptied, g + 2)
                    dve.wait_ge(done, base + 1)
                    v.tensor_copy(high[:], full[:]).then_inc(done, 1)
                    dve.wait_ge(split_out[i], 16 * g2 + 1)
                    v.tensor_copy(split[i][:, :, 0, :], full[:, :, 0, :]).then_inc(done, 1)
                    v.tensor_copy(split[i][0:QB, :, 2, :], full[0:QB, :, 1, :]).then_inc(done, 1)
                    dve.wait_ge(done, base + 4)
                    v.tensor_tensor(split[i][:, :, 1, :], full[:, :, 0, :], f32(high[:, :, 0, :]), ALU.subtract)
                    v.tensor_tensor(split[i][QB:P, :, 2, :], full[QB:P, :, 1, :], f32(high[QB:P, :, 1, :]),
                                    ALU.subtract).then_inc(split_done, 1)
            for t in range(TT):
                if t % UN == 0:
                    dve.wait_ge(x_in[t // UN], 16)
                v.bn_stats(st[:, t, :], x_all[:, t, :]).then_inc(step, 1)
            dve.wait_ge(step, TT)
            for t in range(TT):
                v.bn_aggr(mv[:, t, :], st[:, t, :]).then_inc(step, 1)
            dve.wait_ge(std_done, 1)
            v.reciprocal(rstd[:], std[:]).then_inc(step, 1)
            dve.wait_ge(step, 2 * TT + 1)
            with dve.Fori(0, TT // 2) as t2:
                for i in range(2):
                    t = 2 * t2 + i
                    if i == 0:
                        dve.wait_ge(xn_used, 2 * t2 + 1)
                    v.tensor_scalar(xn[i][:], x_all[:, ds(t, 1), :].rearrange("p o d -> p (o d)"),
                                    mv[:, ds(t, 1), 0], rstd[:, ds(t, 1)], ALU.subtract, ALU.mult).then_inc(xn_ready, 1)
            with dve.Fori(0, NB) as n:
                tok = ds(n * BLK, BLK)
                for j, (src, rows, hi, lo) in enumerate(((kvf, P, "kvTH", "kvTL"), (qaf, P, "qaH", "qaL"), (qbf, QB, "qbH", "qbL"))):
                    dve.wait_ge(proj_out, 3 * n + j + 2)
                    v.tensor_copy(keep[hi][:, tok], src[:]).then_inc(step, 1)
                    dve.wait_ge(step, 2 * TT + 1 + 4 * n + j + 1)
                    v.tensor_tensor(keep[lo][0:rows, tok], src[0:rows, :], f32(keep[hi][0:rows, tok]), ALU.subtract)
                dve.wait_ge(c_done, n + 1)
                v.tensor_copy(keep["c_all"][:, ds(n * NH * UN, NH * UN)].rearrange("p (h u) -> p u h", h=NH),
                              psD[:, 0:UN * NH].rearrange("p (u h) -> p u h", u=UN)).then_inc(c_out, 1)
                dve.wait_ge(n_done, n + 1)
                four = psN[:, 0:UN * KVL].rearrange("p (u c) -> p u c", u=UN)
                v.tensor_copy(keep["kvn"][:, ds(UN * n, UN), 0:KVL], four).then_inc(step, 1)
                dve.wait_ge(step, 2 * TT + 1 + 4 * n + 4)
                v.tensor_tensor(keep["kvn"][:, ds(UN * n, UN), KVL:P], four, f32(keep["kvn"][:, ds(UN * n, UN), 0:KVL]),
                                ALU.subtract).then_inc(c_out, 1)


class Counts:

    @staticmethod
    def filled(g, k):
        if isinstance(g, int):
            if g == -1:
                return 1
            if g == 0:
                return k
            if g == NG - 1 and k > 6:
                return 10 * g + k - 2
            if g == NG:
                return 10 * g + (k - 2 if k < 2 else 0)
        return 10 * g + k - 1

    @staticmethod
    def emptied(g, k):
        if isinstance(g, int):
            if g == -1:
                return 1
            if g == NG or (g == NG - 1 and k > 6):
                return 9 * g + k - 1
        return 9 * g + k


def attention(nc, dram, keep):
    with ExitStack() as ctx:
        sb = lambda n, s, d=F32: ctx.enter_context(nc.sbuf_tensor(n, s, d))
        sem = lambda n: ctx.enter_context(nc.semaphore(n))
        weff = [sb(f"weff{i}", [P, 3, P], F32R) for i in range(2)]
        wv = [sb(f"wv{i}", [P, VH]) for i in range(2)]
        qeH = [sb(f"qeH{i}", [P, BLK], F32R) for i in range(2)]
        qeL = [sb(f"qeL{i}", [P, BLK], F32R) for i in range(2)]
        prob = [sb(f"prob{i}", [P, SEQ]) for i in range(2)]
        PTH = [sb(f"PTH{i}", [P, KEYT, BLK], F32R) for i in range(2)]
        PTL = [sb(f"PTL{i}", [P, KEYT, BLK], F32R) for i in range(2)]
        onorm, rsum_b = sb("onorm", [P, BLK]), sb("rsum_b", [P, BLK])
        mx, shift = sb("mx", [P, 2 * UN]), sb("shift", [P, 2 * UN])
        rs, rinv = sb("rs", [P, 2 * UN]), sb("rinv", [P, UN])
        bv, ones = sb("bv", [NH, VH]), sb("ones_row", [NH, BLK])
        S = ctx.enter_context(nc.psum_tensor("S", [P, 2, SEQ], F32))
        X = ctx.enter_context(nc.psum_tensor("X", [P, 2, BLK], F32))
        O = ctx.enter_context(nc.psum_tensor("O", [P, BLK], F32))
        V = ctx.enter_context(nc.psum_tensor("V", [P, BLK], F32))
        weff_in = [sem(f"weff_in{i}") for i in range(2)]
        wv_in = [sem(f"wv_in{i}") for i in range(2)]
        names = ("bv_in", "ones_set", "scores_ready", "max_ready", "shift_ready", "probs_ready", "x_filled",
                 "high_out", "low_out", "recip_ready", "recip_out", "pv_done", "onorm_ready", "wv_done",
                 "vsum_ready", "vsum_out")
        (bv_in, ones_set, scores_ready, max_ready, shift_ready, probs_ready, x_filled, high_out, low_out,
         recip_ready, recip_out, pv_done, onorm_ready, wv_done, vsum_ready, vsum_out) = (sem(n) for n in names)
        ident = keep["ident"]
        filled, emptied = Counts.filled, Counts.emptied
        block = ctx.enter_context(nc.Block())

        def steps(eng, body, after=0):
            for b in range(NB):
                for h in (0, 1):
                    body(b * NH + h, b, h, h)
                with eng.Fori(1, NH // 2 - 1) as pair:
                    for par in range(2):
                        body(b * NH + 2 * pair + par, b, 2 * pair + par, par)
                for h in (NH - 2, NH - 1):
                    body(b * NH + h, b, h, h % 2)
            for g in range(NG, NG + after):
                body(g, NB, g - NG, g % 2)

        def exists(g):
            return not isinstance(g, int) or 0 <= g < NG

        def half(g, par):
            return g // 2 if isinstance(g, int) else (g - par) // 2

        def last_unit_events(g):
            return [(g, k, UN - 1, k) for k in (0, 1)]

        @block.sync
        def _(sp):
            sp.dma_start(bv[:], dram["bv"]).then_inc(bv_in, 16)

            def load(g, h, par):
                if not isinstance(g, int) or g >= 2:
                    sp.wait_ge(x_filled, filled(g - 3, 6))
                sp.dma_start(f32(weff[par][:].rearrange("p t c -> p (t c)")), dram["weff_h"][h]).then_inc(weff_in[par], 16)

            for b in range(NB):
                for h in range(4):
                    load(b * NH + h, h, h % 2)
                with sp.Fori(2, NH // 2) as pair:
                    for par in range(2):
                        load(b * NH + 2 * pair + par, 2 * pair + par, par)

        @block.gpsimd
        def _(pool):
            nc.gpsimd.memset(ones[:], 1.0).then_inc(ones_set, 1)

            def load(g, h, par):
                if not isinstance(g, int) or g >= 2:
                    pool.wait_ge(wv_done, g - 1)
                pool.dma_start(wv[par][:], dram["wv"][h]).then_inc(wv_in[par], 16)

            for b in range(NB):
                for h in range(2):
                    load(b * NH + h, h, h)
                with pool.Fori(1, NH // 2) as pair:
                    for par in range(2):
                        load(b * NH + 2 * pair + par, 2 * pair + par, par)

        @block.tensor
        def _(pe):
            mm = nc.tensor.matmul

            def project_queries(g, b, par, turn, k):
                pe.wait_ge(weff_in[par], 16 * turn)
                tok = slice(b * BLK, (b + 1) * BLK)
                out = X[:, 0, :]
                w = weff[par]
                mm(out, w[:, 0, :], keep["qaH"][:, tok], start=True, stop=False)
                mm(out, w[:, 0, :], keep["qaL"][:, tok], start=False, stop=False)
                mm(out, w[:, 1, :], keep["qaH"][:, tok], start=False, stop=False)
                mm(out, w[:, 2, :], keep["qbH"][:, tok], start=False, stop=False)
                mm(out, w[0:QB, 2, :], keep["qbL"][0:QB, tok], start=False, stop=True).then_inc(x_filled, 1)

            def transposes(g, unit, k, part):
                for j in range(4):
                    last = nc.tensor.transpose(X[:, k % 2, j * P:(j + 1) * P],
                                               prob[unit % 2][:, (4 * part + j) * P:(4 * part + j + 1) * P], ident[:])
                last.then_inc(x_filled, 1)

            project_queries(0, 0, 0, 1, 6)

            def body(g, b, h, par):
                on = exists(g)
                batch = b // 2

                def scores(u):
                    if u == 0:
                        pe.wait_ge(low_out, emptied(g - 1, 6))
                    if not isinstance(g, int) or 4 * g + u >= 2:
                        pe.wait_ge(probs_ready, 4 * g + u - 1)
                    q = slice(u * P, (u + 1) * P)
                    for c in range(2):
                        keys = slice(batch * SEQ + c * BLK, batch * SEQ + (c + 1) * BLK)
                        out = S[:, u % 2, c * BLK:(c + 1) * BLK]
                        mm(out, qeH[par][:, q], keep["kvTH"][:, keys], start=True, stop=False)
                        mm(out, qeH[par][:, q], keep["kvTL"][:, keys], start=False, stop=False)
                        last = mm(out, qeL[par][:, q], keep["kvTH"][:, keys], start=False, stop=True)
                    last.then_inc(scores_ready, 1)

                def pv(first, last_):
                    kb = ((b * NH + h - 1) // NH if isinstance(h, int) else b) // 2
                    for n in range(first, last_):
                        kt, src = n // 2, (PTH, PTL)[n % 2]
                        ins = mm(O[:], keep["kvn"][:, kb * KEYT + kt, :], src[1 - par][:, kt, :],
                                 start=(n == 0), stop=(n == 2 * KEYT - 1))
                    if last_ == 2 * KEYT:
                        ins.then_inc(pv_done, 1)

                before = exists(g - 1) and not (isinstance(g, int) and g == 0)
                if on:
                    scores(0)
                if before:
                    pe.wait_ge(probs_ready, 4 * g)
                    pe.wait_ge(low_out, emptied(g - 1, 8))
                    transposes(g, UN - 1, 0, 0)
                    if isinstance(g, int) and g == 1:
                        pe.wait_ge(low_out, emptied(0, 7))
                    else:
                        pe.wait_ge(recip_out, g - 1)
                    transposes(g, UN - 1, 1, 1)
                if on:
                    scores(1)
                    pe.wait_ge(probs_ready, 4 * g + 1)
                    pe.wait_ge(low_out, emptied(g - 1, 6) if isinstance(g, int) and g == 0 else emptied(g, 0))
                    transposes(g, 0, 2, 0)
                    if before:
                        pe.wait_ge(low_out, emptied(g, 1))
                    transposes(g, 0, 3, 1)
                if isinstance(h, int) and h == 1 and on:
                    pe.wait_ge(bv_in, 16)
                    pe.wait_ge(ones_set, 1)
                    if b:
                        product(g, b, h, par)
                        pe.wait_ge(vsum_out, b)
                    mm(V[:], bv[:], ones[:], start=True, stop=False)
                elif not isinstance(g, int) or g >= 2:
                    product(g, b, h, par)
                if before:
                    if not isinstance(g, int) or g >= 2:
                        pe.wait_ge(onorm_ready, g - 1)
                    pe.wait_ge(low_out, emptied(g, 1))
                    pv(0, 5)
                if on:
                    scores(2)
                    pe.wait_ge(probs_ready, 4 * g + 2)
                    pe.wait_ge(low_out, emptied(g, 2))
                    transposes(g, 1, 4, 0)
                    pe.wait_ge(low_out, emptied(g, 3))
                    transposes(g, 1, 5, 1)
                    if exists(g + 1):
                        nb, turn = (b, half(g, par) + 1 + par) if not isinstance(g, int) else ((g + 1) // NH, (g + 1) // 2 + 1)
                        pe.wait_ge(low_out, emptied(g, 4))
                        project_queries(g + 1, nb, 1 - par, turn, 6)
                if before:
                    pv(5, 10)
                if on:
                    scores(3)
                    pe.wait_ge(probs_ready, 4 * g + 3)
                    pe.wait_ge(low_out, emptied(g, 5))
                    if exists(g + 1):
                        transposes(g, 2, 7, 0)
                        pe.wait_ge(low_out, emptied(g, 6))
                        transposes(g, 2, 8, 1)
                    else:
                        transposes(g, 2, 7, 0)
                        transposes(g, 2, 8, 1)
                if before:
                    pv(10, 16)
                    pe.wait_ge(recip_ready, g)
                    pe.wait_ge(low_out, emptied(g, 7 if on else 1))
                    for u in range(UN):
                        last = nc.tensor.transpose(X[:, 1, u * P:(u + 1) * P], rinv[:, u:u + 1].to_broadcast([P, P]), ident[:])
                    last.then_inc(x_filled, 1)

            def product(g, b, h, par):
                pe.wait_ge(wv_in[par], 16 * half(g, par))
                pe.wait_ge(onorm_ready, g - 1)
                end = isinstance(h, int) and h == 1
                ins = mm(V[:], wv[par][:], onorm[:], start=False, stop=end)
                ins.then_inc(wv_done, 1)

            steps(pe, body, after=2)

        @block.scalar
        def _(act):
            def high(g, k, out):
                act.wait_ge(x_filled, filled(g, k))
                nc.scalar.activation(out, X[:, k % 2, :].rearrange("p (k c) -> p k c", k=4), ACT.Copy).then_inc(high_out, 1)

            def high_q(g, h, par, k=6):
                act.wait_ge(x_filled, filled(g, k))
                nc.scalar.activation(qeH[par][:], X[:, 0, :], ACT.Identity, bias=keep["beff"][:, ds(h, 1)]).then_inc(high_out, 1)

            high_q(-1, 0, 0)

            def body(g, b, h, par):
                on, before = exists(g), exists(g - 1) and not (isinstance(g, int) and g == 0)

                def exp(u):
                    col = par * UN + u
                    act.wait_ge(shift_ready, 4 * g + u + 1)
                    nc.scalar.activation(prob[u % 2][:], S[:, u % 2, :], ACT.Exp, bias=shift[:, col:col + 1],
                                         accum_out=rs[:, col:col + 1]).then_inc(probs_ready, 1)

                def pt(u, part, p):
                    return PTH[p][:, 4 * part:4 * part + 4, u * P:(u + 1) * P]

                if not isinstance(g, int) or g >= 2:
                    act.wait_ge(x_filled, filled(g - 1, 9))
                    if not isinstance(g, int) or g >= 3:
                        act.wait_ge(onorm_ready, g - 2)
                    nc.scalar.activation(rsum_b[:], X[:, 1, :], ACT.Copy).then_inc(recip_out, 1)
                if before:
                    for part in range(2):
                        high(g, part, pt(UN - 1, part, 1 - par))
                if on:
                    exp(0)
                    if not isinstance(g, int) or g >= 2:
                        act.wait_ge(pv_done, g - 1)
                    for part in range(2):
                        high(g, 2 + part, pt(0, part, par))
                    exp(1)
                    for part in range(2):
                        high(g, 4 + part, pt(1, part, par))
                    if exists(g + 1):
                        nh = h + 1 if not isinstance(g, int) else (h + 1) % NH
                        high_q(g, nh, 1 - par)
                    exp(2)
                    for part in range(2):
                        high(g, 7 + part, pt(2, part, par))
                    exp(3)

            steps(act, body, after=2)

        @block.vector
        def _(dve):
            v = nc.vector

            def low(g, k, u, part, p):
                dve.wait_ge(high_out, emptied(g, k))
                at = (slice(None), slice(4 * part, 4 * part + 4), slice(u * P, (u + 1) * P))
                v.tensor_tensor(PTL[p][at], X[:, k % 2, :].rearrange("p (k c) -> p k c", k=4), f32(PTH[p][at]),
                                ALU.subtract).then_inc(low_out, 1)

            def low_q(g, h, par):
                dve.wait_ge(high_out, emptied(g, 6))
                v.scalar_tensor_tensor(out=qeL[par][:], in0=X[:, 0, :], scalar=keep["beff"][:, ds(h, 1)],
                                       in1=f32(qeH[par][:]), op0=ALU.add, op1=ALU.subtract).then_inc(low_out, 1)

            low_q(-1, 0, 0)

            def body(g, b, h, par):
                on, before = exists(g), exists(g - 1) and not (isinstance(g, int) and g == 0)

                def maximum(u):
                    col = par * UN + u
                    bias = keep["c_all"][:, ds((b * NH + h) * UN + u, 1)]
                    dve.wait_ge(scores_ready, 4 * g + u + 1)
                    v.reduce_max(mx[:, col:col + 1], S[:, u % 2, :], AX.X).then_inc(max_ready, 1)
                    dve.wait_ge(max_ready, 4 * g + u + 1)
                    v.scalar_tensor_tensor(out=shift[:, col:col + 1], in0=mx[:, col:col + 1], scalar=bias, in1=bias,
                                           op0=ALU.add, op1=ALU.subtract, reverse1=True).then_inc(shift_ready, 1)

                if not isinstance(g, int) or g >= 2:
                    dve.wait_ge(pv_done, g - 1)
                    dve.wait_ge(recip_out, g - 1)
                    if not isinstance(g, int) or g >= 3:
                        dve.wait_ge(wv_done, g - 2)
                    v.tensor_tensor(onorm[:], O[:], rsum_b[:], ALU.mult).then_inc(onorm_ready, 1)
                if on:
                    maximum(0)
                if before:
                    for part in range(2):
                        low(g, part, UN - 1, part, 1 - par)
                    dve.wait_ge(probs_ready, 4 * g)
                    v.reciprocal(rinv[:], rs[:, (1 - par) * UN:(2 - par) * UN]).then_inc(recip_ready, 1)
                if on:
                    maximum(1)
                    for part in range(2):
                        low(g, 2 + part, 0, part, par)
                if isinstance(h, int) and h == 1 and b:
                    dve.wait_ge(wv_done, b * NH)
                    v.tensor_copy(keep["vsum"][:, (b - 1) * BLK:b * BLK], V[:]).then_inc(vsum_out, 1)
                if on:
                    maximum(2)
                    for part in range(2):
                        low(g, 4 + part, 1, part, par)
                    if exists(g + 1):
                        nh = h + 1 if not isinstance(g, int) else (h + 1) % NH
                        low_q(g, nh, 1 - par)
                    maximum(3)
                    for part in range(2):
                        low(g, 7 + part, 2, part, par)

            steps(dve, body, after=2)


def feed_forward(nc, dram, keep):
    with ExitStack() as ctx:
        sb = lambda n, s, d=F32: ctx.enter_context(nc.sbuf_tensor(n, s, d))
        sem = lambda n: ctx.enter_context(nc.semaphore(n))
        kraw = sb("kraw", [P, 3, KT, HID], U8)
        w = sb("ffn_w", [P, 3, KT, HID], F32R)
        wo, bo = sb("wo", [P, HID]), sb("bo", [P, HID])
        sc, sc2 = sb("sc", [P, 3]), sb("sc2", [P, 3])
        row, row2 = sb("row", [P, KT]), sb("row2", [P, KT, 2])
        eps, spare = sb("eps4", [P, 1]), sb("spare", [P, 1])
        vs = sb("vs", [P, BLK])
        x1, y = sb("x1", [P, UN, HID]), sb("y", [P, UN, HID])
        xn2 = sb("xn2", [P, UN, HID])
        st, mv, std, rstd = sb("st4", [P, UN, 6]), sb("mv4", [P, UN, 2]), sb("std4", [P, UN]), sb("rstd4", [P, UN])
        aH = [sb(f"aH{i}", [P, KT, BLK], F32R) for i in range(2)]
        aL = [sb(f"aL{i}", [P, KT, BLK], F32R) for i in range(2)]
        hf = [sb(f"hf{i}", [P, BLK]) for i in range(2)]
        B = [ctx.enter_context(nc.psum_tensor(f"B{i}", [P, 512], F32)) for i in range(4)]
        names = ("c_in", "x4_in", "vs_ready", "mm_done", "const4", "w_ready", "biased", "summed", "stats", "std4_done",
                 "rstd4_done", "normed", "high_in", "split_in", "relu_done", "high_h", "split_h", "y_done", "stored")
        (c_in, x_in, vs_ready, mm_done, const, w_ready, biased, summed, stats, std_done, rstd_done, normed, high_in,
         split_in, relu_done, high_h, split_h, y_done, stored) = (sem(n) for n in names)
        ident = keep["ident"]
        MM = 20
        block = ctx.enter_context(nc.Block())

        @block.sync
        def _(sp):
            sp.dma_start(wo[:], dram["woT"]).then_inc(c_in, 16)
            sp.dma_start(bo[:], dram["bo"].partition_broadcast(P)).then_inc(c_in, 16)
            for j in range(3):
                sp.dma_start(kraw[:, j], dram[f"k{j}"].rearrange("(k p) n -> p k n", p=P)).then_inc(c_in, 16)
                sp.dma_start(sc[:, j:j + 1], dram[f"s{j}"].partition_broadcast(P)).then_inc(c_in, 16)
            with sp.Fori(0, NB) as n:
                sp.wait_ge(stored, 16 * n + 1)
                sp.dma_start(x1[:], dram["x"][ds(n * BLK, BLK), :].rearrange("(t p) d -> p t d", p=P)).then_inc(x_in, 16)
                sp.wait_ge(y_done, UN * n + UN + 1)
                sp.dma_start(dram["out"][ds(n * BLK, BLK), :].rearrange("(t p) d -> p t d", p=P), y[:]).then_inc(stored, 16)
            sp.wait_ge(stored, 16 * NB + 1)

        @block.gpsimd
        def _(pool):
            for free in (stored, y_done, mm_done):
                pool.sem_inc(free, 1)
            nc.gpsimd.memset(row[:], 1.0).then_inc(const, 1)
            nc.gpsimd.memset(eps[:], EPS).then_inc(const, 1)
            pool.wait_ge(const, 2)
            nc.gpsimd.affine_select(out=row[:], in_=row[:], compare_op=ALU.is_ge, fill=INH, base=EXC - 1,
                                    pattern=[[-P, KT]], channel_multiplier=-1).then_inc(const, 1)

        @block.tensor
        def _(pe):
            mm = nc.tensor.matmul
            pe.wait_ge(c_in, 128)
            with pe.Fori(0, NB) as n:
                pe.wait_ge(vs_ready, n + 1)
                pe.wait_ge(y_done, UN * n + 1)
                for t in range(UN):
                    mm(B[t][:], vs[:, t * P:(t + 1) * P], wo[:], start=True, stop=True).then_inc(mm_done, 1)
                pe.wait_ge(normed, UN * n + UN)
                for k in range(KT):
                    for t in range(UN):
                        last = nc.tensor.transpose(B[k][:, t * P:(t + 1) * P], xn2[:, t, k * P:(k + 1) * P], ident[:])
                    last.then_inc(mm_done, 1)
                pe.wait_ge(w_ready, 1)
                pe.wait_ge(split_in, KT * n + KT)
                for layer in range(2):
                    if layer:
                        pe.wait_ge(split_h, 2 * KT * n + KT)
                    for m in range(KT):
                        cols = slice(m * P, (m + 1) * P)
                        for k in range(KT):
                            mm(B[m][:], w[:, layer, k, cols], aH[layer][:, k, :], start=(k == 0), stop=False)
                            last = mm(B[m][:], w[:, layer, k, cols], aL[layer][:, k, :], start=False, stop=(k == KT - 1))
                        last.then_inc(mm_done, 1)
                pe.wait_ge(split_h, 2 * KT * n + 2 * KT)
                for t in range(UN):
                    tok = slice(t * P, (t + 1) * P)
                    for k in range(KT):
                        mm(B[t][:], aH[0][:, k, tok], w[:, 2, k, :], start=(k == 0), stop=False)
                        last = mm(B[t][:], aL[0][:, k, tok], w[:, 2, k, :], start=False, stop=(k == KT - 1))
                    last.then_inc(mm_done, 1)

        @block.scalar
        def _(act):
            act.wait_ge(const, 4)
            with act.Fori(0, NB) as n:
                act.wait_ge(mm_done, 1 + MM * n)
                nc.scalar.activation(vs[:], keep["vsum"][:, ds(n * BLK, BLK)], ACT.Copy).then_inc(vs_ready, 1)
                act.wait_ge(stats, 2 * UN * n + 2 * UN)
                nc.scalar.activation(std[:], mv[:, :, 1], ACT.Sqrt, bias=eps[:]).then_inc(std_done, 1)
                for k in range(KT):
                    act.wait_ge(mm_done, 1 + MM * n + UN + k + 1)
                    nc.scalar.activation(aH[0][:, k, :], B[k][:], ACT.Copy).then_inc(high_in, 1)
                for i in range(2 * KT):
                    layer, m = divmod(i, KT)
                    act.wait_ge(mm_done, 1 + MM * n + 8 + i + 1)
                    if i >= 2:
                        act.wait_ge(split_h, 2 * KT * n + i - 1)
                    nc.scalar.activation(hf[m % 2][:], B[m][:], ACT.Relu, scale=sc2[:, layer:layer + 1]).then_inc(relu_done, 1)

        @block.vector
        def _(dve):
            v = nc.vector
            dve.wait_ge(c_in, 128)
            dve.wait_ge(const, 3)
            v.tensor_scalar(sc2[:], sc[:], 2.0, None, ALU.mult)
            v.tensor_scalar(row2[:, :, 0], row[:], 2.0, None, ALU.mult)
            v.tensor_scalar(row2[:, :, 1], row[:], -1.0, None, ALU.mult).then_inc(const, 1)
            dve.wait_ge(const, 4)
            v.tensor_scalar(w[:, 0], kraw[:, 0], 2.0, -1.0, ALU.mult, ALU.add)
            for j in (1, 2):
                for k in range(KT):
                    last = v.tensor_scalar(w[:, j, k, :], kraw[:, j, k, :], row2[:, k, 0:1], row2[:, k, 1:2], ALU.mult, ALU.add)
            last.then_inc(w_ready, 1)
            with dve.Fori(0, NB) as n:
                dve.wait_ge(x_in, 16 * n + 16)
                for t in range(UN):
                    dve.wait_ge(mm_done, 1 + MM * n + t + 1)
                    v.tensor_tensor(y[:, t, :], B[t][:], bo[:], ALU.add).then_inc(biased, 1)
                dve.wait_ge(biased, UN * n + UN)
                v.tensor_tensor(x1[:], x1[:], y[:], ALU.add).then_inc(summed, 1)
                dve.wait_ge(summed, n + 1)
                for t in range(UN):
                    v.bn_stats(st[:, t, :], x1[:, t, :]).then_inc(stats, 1)
                dve.wait_ge(stats, 2 * UN * n + UN)
                v.memset(spare[:], 0.0)
                for t in range(UN):
                    v.bn_aggr(mv[:, t, :], st[:, t, :]).then_inc(stats, 1)
                dve.wait_ge(std_done, n + 1)
                v.reciprocal(rstd[:], std[:]).then_inc(rstd_done, 1)
                dve.wait_ge(rstd_done, n + 1)
                for t in range(UN):
                    v.tensor_scalar(xn2[:, t, :], x1[:, t, :], mv[:, t, 0:1], rstd[:, t:t + 1], ALU.subtract,
                                    ALU.mult).then_inc(normed, 1)
                for k in range(KT):
                    dve.wait_ge(high_in, KT * n + k + 1)
                    v.tensor_tensor(aL[0][:, k, :], B[k][:], f32(aH[0][:, k, :]), ALU.subtract).then_inc(split_in, 1)
                for i in range(2 * KT):
                    layer, m = divmod(i, KT)
                    to = 1 - layer
                    dve.wait_ge(relu_done, 2 * KT * n + i + 1)
                    v.tensor_copy(aH[to][:, m, :], hf[m % 2][:]).then_inc(high_h, 1)
                    dve.wait_ge(high_h, 2 * KT * n + i + 1)
                    v.tensor_tensor(aL[to][:, m, :], hf[m % 2][:], f32(aH[to][:, m, :]), ALU.subtract).then_inc(split_h, 1)
                for t in range(UN):
                    dve.wait_ge(mm_done, 1 + MM * n + 16 + t + 1)
                    v.scalar_tensor_tensor(out=y[:, t, :], in0=B[t][:], scalar=sc[:, 2:3], in1=x1[:, t, :],
                                           op0=ALU.mult, op1=ALU.add).then_inc(y_done, 1)


def layer(nc, dram):
    with ExitStack() as ctx:
        sb = lambda n, s, d=F32: ctx.enter_context(nc.sbuf_tensor(n, s, d))
        keep = {
            "ident": sb("ident", [P, P]), "beff": sb("beff", [P, NH]), "c_all": sb("c_all", [P, NG * UN]),
            "kvTH": sb("kvTH", [P, TOK], F32R), "kvTL": sb("kvTL", [P, TOK], F32R),
            "kvn": sb("kvn", [P, TT, P], F32R),
            "qaH": sb("qaH", [P, TOK], F32R), "qaL": sb("qaL", [P, TOK], F32R),
            "qbH": sb("qbH", [P, TOK], F32R), "qbL": sb("qbL", [P, TOK], F32R),
            "vsum": sb("vsum", [P, TOK]),
        }
        prepare(nc, dram, keep)
        attention(nc, dram, keep)
        feed_forward(nc, dram, keep)


def laid_out(a):
    t = lambda n: np.asarray(a["L0_attn_" + n])
    wq = t("Wq_up").reshape(NH, QHEAD, QL)
    bq = t("bq_up").reshape(NH, QHEAD)
    wkv = t("Wkv_up").reshape(NH, NOPE + VH, KVL)
    bkv = t("bkv_up").reshape(NH, NOPE + VH)
    twice = np.r_[0:P, P:QL, P:QL]
    raw = np.concatenate([wq[:, :NOPE][:, :, twice], wkv[:, :NOPE], bkv[:, :NOPE, None], bq[:, :NOPE, None],
                          wq[:, NOPE:].transpose(0, 2, 1)[:, 0:P],
                          wq[:, NOPE:].transpose(0, 2, 1)[:, np.r_[P:QL, P:QL]]], axis=2)
    wvT = wkv[:, NOPE:].transpose(0, 2, 1)
    bqc = t("bq_c")
    out = {
        "x": t("hidden_size").reshape(TOK, HID),
        "raw": raw.reshape(NH // HG, HG, P, R_N).transpose(0, 2, 1, 3).reshape(NH // HG, P, HG * R_N),
        "bqrT": bq[:, NOPE:].T,
        "wqcT": t("Wq_c").T[:, twice], "wkvcT": t("Wkv_c").T,
        "pb": np.stack([t("bkv_c"), bqc[:P], bqc[np.r_[P:QL, P:QL]]], axis=1),
        "wv": np.concatenate([wvT, wvT], axis=1), "bv": bkv[:, NOPE:],
        "woT": t("Wo").T, "bo": t("bo"),
    }
    for j in range(3):
        out[f"k{j}"] = np.asarray(a[f"L0_ffn_k{j}"])
        out[f"s{j}"] = np.asarray(a[f"L0_ffn_s{j}"]).reshape(1)
    return {n: np.ascontiguousarray(v) for n, v in out.items()}


def kernel(**inputs):
    import concourse.bacc as bacc
    from concourse.bass_utils import run_bass_kernel_spmd

    nc = bacc.Bacc("TRN2", target_bir_lowering=False, num_devices=1)
    arrays = laid_out(inputs)
    dram = {n: nc.dram_tensor("in_" + n, v.shape, mybir.dt.from_np(v.dtype), kind="ExternalInput").ap()
            for n, v in arrays.items()}
    dram["out"] = nc.dram_tensor("out", (TOK, HID), F32, kind="ExternalOutput").ap()
    dram["weff"] = nc.dram_tensor("weff_scratch", (NH // HG, HG, P, 3 * P), F32, kind="Internal").ap()
    dram["weff_h"] = dram["weff"].rearrange("g h p c -> (g h) p c")
    layer(nc, dram)
    r = run_bass_kernel_spmd(nc, [{"in_" + n: v for n, v in arrays.items()}], core_ids=[0])
    return r.results[0]["out"].reshape(BATCH, SEQ, HID)
```

```python
from contextlib import ExitStack

import numpy as np
import concourse.bass as bass
from concourse import mybir

F32 = mybir.dt.float32
F32R = mybir.dt.float32r
U8 = mybir.dt.uint8
ACT = mybir.ActivationFunctionType
ALU = mybir.AluOpType
AX = mybir.AxisListType
ds = bass.ds

P = 128
NH = 32
NOPE, ROPE, VH = 128, 64, 128
QHEAD = NOPE + ROPE
QL, KVL = 192, 64
QB = QL - P
HID = 512
KT = HID // P
BATCH, SEQ = 2, 1024
TOK = BATCH * SEQ
TT = TOK // P
BLK = 512
NB = TOK // BLK
UN = BLK // P
KEYT = SEQ // P
NG = NB * NH
EPS = 1e-5
SCALE = float(1.0 / np.sqrt(QHEAD))
EXC = round(HID * 0.8)
INH = float(np.float32(-0.8 / (1.0 - 0.8)))
R_WK, R_BK, R_BQ, R_QR, R_N = 256, 320, 321, 322, 450
HG = 4


def f32(ap):
    return ap.bitcast(F32)


def prepare(nc, dram, keep):
    with ExitStack() as ctx:
        sb = lambda n, s, d=F32: ctx.enter_context(nc.sbuf_tensor(n, s, d))
        ps = lambda n: ctx.enter_context(nc.psum_tensor(n, [P, 512], F32))
        sem = lambda n: ctx.enter_context(nc.semaphore(n))
        raw = [sb(f"raw{i}", [P, HG, R_N]) for i in range(2)]
        full = sb("w_full", [P, HG, 2, P])
        high = sb("w_high", [P, HG, 2, P], F32R)
        split = [sb(f"w_split{i}", [P, HG, 3, P], F32R) for i in range(2)]
        wcA, wcB, bqk = sb("wcA", [P, NH]), sb("wcB", [P, NH]), sb("bqk", [P, NH])
        bqr = sb("bqr", [P, NH])
        x_all = sb("x_all", [P, TT, HID])
        xn = [sb(f"xn{i}", [P, HID]) for i in range(2)]
        xnT = sb("xnT", [P, KT, TOK])
        wqc, wkvc = sb("wqc", [P, KT, 2 * P]), sb("wkvc", [P, KT, P])
        pb = sb("proj_bias", [P, 3])
        st, mv = sb("st", [P, TT, 6]), sb("mv", [P, TT, 2])
        std, rstd = sb("std", [P, TT]), sb("rstd", [P, TT])
        eps, ones = sb("eps", [P, 1]), sb("ones", [P, P])
        kvf, qaf, qbf = sb("kvf", [P, BLK]), sb("qaf", [P, BLK]), sb("qbf", [P, BLK])
        psA, psB, psC = ps("psA"), ps("psB"), ps("psC")
        psT = [ps("psT0"), ps("psT1")]
        psN, psD = ps("psN"), ps("psD")
        raw_in = [sem(f"raw_in{i}") for i in range(2)]
        split_out = [sem(f"split_out{i}") for i in range(2)]
        x_in = [sem(f"x_in{i}") for i in range(NB)]
        bias_in, w_in, absorbed, emptied, split_done, const = (
            sem(n) for n in ("bias_in", "w_in", "absorbed", "emptied", "split_done", "const"))
        step, std_done, xn_ready, xn_used, xnT_ready = (
            sem(n) for n in ("step", "std_done", "xn_ready", "xn_used", "xnT_ready"))
        proj_done, proj_out, c_done, n_done, c_out = (
            sem(n) for n in ("proj_done", "proj_out", "c_done", "n_done", "c_out"))
        groups = NH // HG
        W = 66
        vA = psA[:, 0:HG * W].rearrange("p (h c) -> p h c", c=W)
        vB = psB[:, 0:HG * W].rearrange("p (h c) -> p h c", c=W)
        vC = psC[:, 0:HG * 2].rearrange("p (h c) -> p h c", c=2)
        ident = keep["ident"]
        block = ctx.enter_context(nc.Block())

        @block.gpsimd
        def _(pool):
            for free in (emptied, xnT_ready, proj_out, c_out, split_done, xn_used, *split_out):
                pool.sem_inc(free, 1)
            nc.gpsimd.memset(ident[:], 0.0).then_inc(const, 1)
            nc.gpsimd.memset(ones[:], 1.0).then_inc(const, 1)
            nc.gpsimd.memset(eps[:], EPS).then_inc(const, 1)
            pool.wait_ge(const, 3)
            nc.gpsimd.affine_select(out=ident[:], in_=ident[:], compare_op=ALU.not_equal, fill=1.0, base=0,
                                    pattern=[[-1, P]], channel_multiplier=1).then_inc(const, 1)

        @block.sync
        def _(sp):
            def load(g, i):
                sp.dma_start(raw[i][:], dram["raw"][g].rearrange("p (h c) -> p h c", h=HG)).then_inc(raw_in[i], 16)

            def store(g, i):
                sp.dma_start(dram["weff"][g].rearrange("h p c -> p h c"),
                             f32(split[i][:].rearrange("p h t c -> p h (t c)"))).then_inc(split_out[i], 16)

            load(0, 0)
            load(1, 1)
            sp.dma_start(bqr[P - ROPE:P, :], dram["bqrT"]).then_inc(bias_in, 16)
            for n in range(NB):
                sp.dma_start(x_all[:, UN * n:UN * (n + 1), :],
                             dram["x"][n * BLK:(n + 1) * BLK, :].rearrange("(t p) d -> p t d", p=P)).then_inc(x_in[n], 16)
            sp.dma_start(wqc[:], dram["wqcT"].rearrange("(k p) c -> p k c", p=P)).then_inc(w_in, 16)
            sp.dma_start(wkvc[:], dram["wkvcT"].rearrange("(k p) c -> p k c", p=P)).then_inc(w_in, 16)
            sp.dma_start(pb[:], dram["pb"]).then_inc(w_in, 16)
            with sp.Fori(0, groups // 2 - 1) as g2:
                for i in range(2):
                    sp.wait_ge(split_done, 2 * g2 + i + 2)
                    store(2 * g2 + i, i)
                    load(2 * g2 + i + 2, i)
            for i in range(2):
                sp.wait_ge(split_done, groups + i)
                store(groups - 2 + i, i)
            for i in range(2):
                sp.wait_ge(split_out[i], 16 * (groups // 2) + 1)

        @block.tensor
        def _(pe):
            mm = nc.tensor.matmul
            with pe.Fori(0, groups // 2) as g2:
                for i in range(2):
                    pe.wait_ge(raw_in[i], 16 * (g2 + 1))
                    pe.wait_ge(emptied, 2 * g2 + i + 1)
                    for h in range(HG):
                        right = raw[i][:, h, R_WK:R_WK + W]
                        mm(vA[:, h, :], raw[i][:, h, 0:P], right, start=True, stop=True)
                        mm(vB[:, h, :], raw[i][:, h, P:2 * P], right, start=True, stop=True)
                        last = mm(vC[0:KVL, h, :], raw[i][:, h, R_WK:R_BK], raw[i][:, h, R_BK:R_QR],
                                  start=True, stop=True)
                    last.then_inc(absorbed, 1)
            pe.wait_ge(const, 4)
            with pe.Fori(0, TT // 2) as t2:
                for i in range(2):
                    if i == 0:
                        pe.wait_ge(xnT_ready, 2 * t2 + 1)
                    pe.wait_ge(xn_ready, 2 * t2 + i + 1)
                    for k in range(KT):
                        last = nc.tensor.transpose(psT[i][:, k * P:(k + 1) * P], xn[i][:, k * P:(k + 1) * P], ident[:])
                    last.then_inc(xn_used, 1)
            pe.wait_ge(xnT_ready, TT + 1)
            pe.wait_ge(w_in, 48)
            with pe.Fori(0, NB) as n:
                pe.wait_ge(proj_out, 3 * n + 1)
                for out, w, c in ((psA, wkvc, 0), (psB, wqc, 0), (psC, wqc, P)):
                    for k in range(KT):
                        last = mm(out[:], w[:, k, c:c + P], xnT[:, k, ds(n * BLK, BLK)], start=(k == 0), stop=(k == KT - 1))
                    last.then_inc(proj_done, 1)
                pe.wait_ge(proj_out, 3 * n + 4)
                pe.wait_ge(c_out, 2 * n + 1)
                for u in range(UN):
                    tok = slice(u * P, (u + 1) * P)
                    out = psD[:, u * NH:(u + 1) * NH]
                    mm(out, qaf[:, tok], wcA[:], start=True, stop=False)
                    mm(out, qbf[0:QB, tok], wcB[0:QB, :], start=False, stop=False)
                    last = mm(out, ones[:], bqk[:], start=False, stop=True)
                last.then_inc(c_done, 1)
                for u in range(UN):
                    tok = slice(u * P, (u + 1) * P)
                    last = nc.tensor.transpose(psN[:, u * KVL:(u + 1) * KVL], kvf[0:KVL, tok], ident[0:KVL, 0:KVL])
                last.then_inc(n_done, 1)

        @block.scalar
        def _(act):
            with act.Fori(0, groups // 2) as g2:
                for i in range(2):
                    act.wait_ge(absorbed, 2 * g2 + i + 1)
                    act.wait_ge(split_done, 2 * g2 + i + 1)
                    heads = ds((2 * g2 + i) * HG, HG)
                    nc.scalar.activation(full[:, :, 0, 0:KVL], vA[:, :, 0:KVL], ACT.Copy, scale=SCALE)
                    nc.scalar.activation(full[:, :, 1, 0:KVL], vB[:, :, 0:KVL], ACT.Copy, scale=SCALE)
                    nc.scalar.activation(wcA[:, heads], vA[:, :, KVL], ACT.Copy, scale=SCALE)
                    nc.scalar.activation(wcB[:, heads], vB[:, :, KVL], ACT.Copy, scale=SCALE)
                    nc.scalar.activation(keep["beff"][0:KVL, heads], vC[0:KVL, :, 1], ACT.Copy,
                                         scale=SCALE).then_inc(emptied, 1)
            act.wait_ge(step, TT * 2)
            act.wait_ge(const, 3)
            nc.scalar.activation(std[:], mv[:, :, 1], ACT.Sqrt, bias=eps[:]).then_inc(std_done, 1)
            with act.Fori(0, TT // 2) as t2:
                for i in range(2):
                    act.wait_ge(xn_used, 2 * t2 + i + 2)
                    nc.scalar.activation(xnT[:, :, ds((2 * t2 + i) * P, P)],
                                         psT[i][:].rearrange("p (k c) -> p k c", k=KT), ACT.Copy).then_inc(xnT_ready, 1)
            act.wait_ge(w_in, 48)
            with act.Fori(0, NB) as n:
                act.wait_ge(c_out, 2 * n + 1)
                for j, (out, src) in enumerate(((kvf, psA), (qaf, psB), (qbf, psC))):
                    act.wait_ge(proj_done, 3 * n + j + 1)
                    nc.scalar.activation(out[:], src[:], ACT.Identity, bias=pb[:, j:j + 1]).then_inc(proj_out, 1)

        @block.vector
        def _(dve):
            v = nc.vector
            done = sem("dve_done")
            count = [0]

            def link(ins):
                count[0] += 1
                ins.then_inc(done, 1)
                dve.wait_ge(done, count[0])

            dve.wait_ge(bias_in, 16)
            link(v.tensor_scalar(keep["beff"][KVL:P, :], bqr[KVL:P, :], SCALE, None, ALU.mult))
            per = 4
            with dve.Fori(0, groups // 2) as g2:
                for i in range(2):
                    g = 2 * g2 + i
                    base = 1 + per * g
                    dve.wait_ge(split_done, g + 1)
                    heads = ds(g * HG, HG)
                    dve.wait_ge(raw_in[i], 16 * (g2 + 1))
                    v.scalar_tensor_tensor(out=bqk[:, heads], in0=raw[i][:, :, R_BK], scalar=SCALE,
                                           in1=raw[i][:, :, R_BQ], op0=ALU.mult, op1=ALU.mult)
                    v.tensor_scalar(full[:, :, :, KVL:P], raw[i][:, :, R_QR:R_N].rearrange("p h (s c) -> p h s c", s=2),
                                    SCALE, None, ALU.mult).then_inc(done, 1)
                    dve.wait_ge(emptied, g + 2)
                    dve.wait_ge(done, base + 1)
                    v.tensor_copy(high[:], full[:]).then_inc(done, 1)
                    dve.wait_ge(split_out[i], 16 * g2 + 1)
                    v.tensor_copy(split[i][:, :, 0, :], full[:, :, 0, :]).then_inc(done, 1)
                    v.tensor_copy(split[i][0:QB, :, 2, :], full[0:QB, :, 1, :]).then_inc(done, 1)
                    dve.wait_ge(done, base + 4)
                    v.tensor_tensor(split[i][:, :, 1, :], full[:, :, 0, :], f32(high[:, :, 0, :]), ALU.subtract)
                    v.tensor_tensor(split[i][QB:P, :, 2, :], full[QB:P, :, 1, :], f32(high[QB:P, :, 1, :]),
                                    ALU.subtract).then_inc(split_done, 1)
            for t in range(TT):
                if t % UN == 0:
                    dve.wait_ge(x_in[t // UN], 16)
                v.bn_stats(st[:, t, :], x_all[:, t, :]).then_inc(step, 1)
            dve.wait_ge(step, TT)
            for t in range(TT):
                v.bn_aggr(mv[:, t, :], st[:, t, :]).then_inc(step, 1)
            dve.wait_ge(std_done, 1)
            v.reciprocal(rstd[:], std[:]).then_inc(step, 1)
            dve.wait_ge(step, 2 * TT + 1)
            with dve.Fori(0, TT // 2) as t2:
                for i in range(2):
                    t = 2 * t2 + i
                    if i == 0:
                        dve.wait_ge(xn_used, 2 * t2 + 1)
                    v.tensor_scalar(xn[i][:], x_all[:, ds(t, 1), :].rearrange("p o d -> p (o d)"),
                                    mv[:, ds(t, 1), 0], rstd[:, ds(t, 1)], ALU.subtract, ALU.mult).then_inc(xn_ready, 1)
            with dve.Fori(0, NB) as n:
                tok = ds(n * BLK, BLK)
                for j, (src, rows, hi, lo) in enumerate(((kvf, P, "kvTH", "kvTL"), (qaf, P, "qaH", "qaL"), (qbf, QB, "qbH", "qbL"))):
                    dve.wait_ge(proj_out, 3 * n + j + 2)
                    v.tensor_copy(keep[hi][:, tok], src[:]).then_inc(step, 1)
                    dve.wait_ge(step, 2 * TT + 1 + 4 * n + j + 1)
                    v.tensor_tensor(keep[lo][0:rows, tok], src[0:rows, :], f32(keep[hi][0:rows, tok]), ALU.subtract)
                dve.wait_ge(c_done, n + 1)
                v.tensor_copy(keep["c_all"][:, ds(n * NH * UN, NH * UN)].rearrange("p (h u) -> p u h", h=NH),
                              psD[:, 0:UN * NH].rearrange("p (u h) -> p u h", u=UN)).then_inc(c_out, 1)
                dve.wait_ge(n_done, n + 1)
                four = psN[:, 0:UN * KVL].rearrange("p (u c) -> p u c", u=UN)
                v.tensor_copy(keep["kvn"][:, ds(UN * n, UN), 0:KVL], four).then_inc(step, 1)
                dve.wait_ge(step, 2 * TT + 1 + 4 * n + 4)
                v.tensor_tensor(keep["kvn"][:, ds(UN * n, UN), KVL:P], four, f32(keep["kvn"][:, ds(UN * n, UN), 0:KVL]),
                                ALU.subtract).then_inc(c_out, 1)


def event(g, k):
    if isinstance(g, int):
        if g == -1:
            return 1
        if g == NG or (g == NG - 1 and k > 6):
            return 9 * g + k - 3
    return 9 * g + k - 2


def bank(g, k, par):
    return event(g, k) % 2 if isinstance(g, int) else (par + k) % 2


def attention(nc, dram, keep):
    with ExitStack() as ctx:
        sb = lambda n, s, d=F32: ctx.enter_context(nc.sbuf_tensor(n, s, d))
        sem = lambda n: ctx.enter_context(nc.semaphore(n))
        weff = [sb(f"weff{i}", [P, 3, P], F32R) for i in range(2)]
        wv = [sb(f"wv{i}", [P, VH]) for i in range(2)]
        qeH = [sb(f"qeH{i}", [P, BLK], F32R) for i in range(2)]
        qeL = [sb(f"qeL{i}", [P, BLK], F32R) for i in range(2)]
        prob = [sb(f"prob{i}", [P, SEQ]) for i in range(UN)]
        PTH = [sb(f"PTH{i}", [P, KEYT, BLK], F32R) for i in range(2)]
        PTL = [sb(f"PTL{i}", [P, KEYT, BLK], F32R) for i in range(2)]
        onorm = sb("onorm", [P, BLK])
        recip_row = [sb(f"recip_row{i}", [P, BLK]) for i in range(2)]
        mx, shift, rs, recip = (sb(n, [P, 2 * UN]) for n in ("mx", "shift", "rs", "recip"))
        bv, ones = sb("bv", [NH, VH]), sb("ones_row", [NH, BLK])
        S = ctx.enter_context(nc.psum_tensor("S", [P, 2, SEQ], F32))
        X = ctx.enter_context(nc.psum_tensor("X", [P, 2, BLK], F32))
        O = ctx.enter_context(nc.psum_tensor("O", [P, BLK], F32))
        V = ctx.enter_context(nc.psum_tensor("V", [P, BLK], F32))
        weff_in = [sem(f"weff_in{i}") for i in range(2)]
        wv_in = [sem(f"wv_in{i}") for i in range(2)]
        row_in = [sem(f"row_in{i}") for i in range(2)]
        names = ("bv_in", "ones_set", "scores_ready", "max_ready", "shift_ready", "probs_ready", "x_filled",
                 "high_out", "low_out", "recip_ready", "recip_out", "pv_done", "onorm_ready", "wv_done", "vsum_out")
        (bv_in, ones_set, scores_ready, max_ready, shift_ready, probs_ready, x_filled, high_out, low_out,
         recip_ready, recip_out, pv_done, onorm_ready, wv_done, vsum_out) = (sem(n) for n in names)
        ident = keep["ident"]
        block = ctx.enter_context(nc.Block())

        def steps(eng, body, after=2):
            for b in range(NB):
                for h in (0, 1):
                    body(b * NH + h, b, h, h)
                with eng.Fori(1, NH // 2 - 1) as pair:
                    for par in range(2):
                        body(b * NH + 2 * pair + par, b, 2 * pair + par, par)
                for h in (NH - 2, NH - 1):
                    body(b * NH + h, b, h, h % 2)
            for g in range(NG, NG + after):
                body(g, NB, g - NG, g % 2)

        def exists(g):
            return not isinstance(g, int) or 0 <= g < NG

        def turns(g, par):
            return g // 2 + 1 if isinstance(g, int) else (g - par) // 2 + 1

        @block.sync
        def _(sp):
            def load(g, weights, par):
                if not isinstance(g, int) or g >= 2:
                    sp.wait_ge(x_filled, event(g - 3, 6))
                sp.dma_start(f32(weff[par][:].rearrange("p t c -> p (t c)")), weights).then_inc(weff_in[par], 16)

            load(0, dram["weff_h"][0], 0)
            load(1, dram["weff_h"][1], 1)
            two_on = dram["weff_h"][2:NH]
            sp.dma_start(bv[:], dram["bv"]).then_inc(bv_in, 16)

            def body(g, b, h, par):
                if exists(g - 1):
                    last = 1 - par
                    sp.wait_ge(recip_ready, g)
                    with nc.allow_non_contiguous_dma(reason="512 numbers, turned from columns into a row"):
                        sp.dma_start(dram["row"][last].rearrange("(u p) -> p u", p=P),
                                     recip[:, last * UN:(last + 1) * UN]).then_inc(recip_out, 16)
                    sp.wait_ge(recip_out, 16 * g)
                    sp.dma_start(recip_row[last][:], dram["row"][last].partition_broadcast(P)).then_inc(row_in[last], 16)
                if exists(g + 2):
                    load(g + 2, two_on[h] if not isinstance(g, int) else dram["weff_h"][(h + 2) % NH], par)

            steps(sp, body, after=1)

        @block.gpsimd
        def _(pool):
            nc.gpsimd.memset(ones[:], 1.0).then_inc(ones_set, 1)

            def load(g, b, h, par):
                if not isinstance(g, int) or g >= 2:
                    pool.wait_ge(wv_done, g - 1)
                pool.dma_start(wv[par][:], dram["wv"][h]).then_inc(wv_in[par], 16)

            steps(pool, load, after=0)

        @block.tensor
        def _(pe):
            mm = nc.tensor.matmul

            def free_bank(g, k, par):
                if not isinstance(g, int) or event(g, k) > 2:
                    pe.wait_ge(low_out, event(g, k) - 2)
                return X[:, bank(g, k, par), :]

            def project_queries(g, par):
                out = free_bank(g, 6, par)
                nxt = g + 1
                pe.wait_ge(weff_in[1 - par], 16 * turns(nxt, 1 - par))
                b = nxt // NH if isinstance(g, int) else block_now[0]
                tok = slice(b * BLK, (b + 1) * BLK)
                w = weff[1 - par]
                mm(out, w[:, 0, :], keep["qaH"][:, tok], start=True, stop=False)
                mm(out, w[:, 0, :], keep["qaL"][:, tok], start=False, stop=False)
                mm(out, w[:, 1, :], keep["qaH"][:, tok], start=False, stop=False)
                mm(out, w[:, 2, :], keep["qbH"][:, tok], start=False, stop=False)
                mm(out, w[0:QB, 2, :], keep["qbL"][0:QB, tok], start=False, stop=True).then_inc(x_filled, 1)

            def transposes(g, par, unit, k, part):
                out = free_bank(g, k, par)
                for j in range(4):
                    last = nc.tensor.transpose(out[:, j * P:(j + 1) * P],
                                               prob[unit][:, (4 * part + j) * P:(4 * part + j + 1) * P], ident[:])
                last.then_inc(x_filled, 1)

            block_now = [0]
            project_queries(-1, 1)

            def body(g, b, h, par):
                block_now[0] = b
                on, one, two = exists(g), exists(g - 1), exists(g - 2)

                def scores(u):
                    if u == 0:
                        pe.wait_ge(low_out, event(g - 1, 6))
                    if not isinstance(g, int) or 4 * g + u >= 2:
                        pe.wait_ge(probs_ready, 4 * g + u - 1)
                    q = slice(u * P, (u + 1) * P)
                    for c in range(2):
                        keys = slice((b // 2) * SEQ + c * BLK, (b // 2) * SEQ + (c + 1) * BLK)
                        out = S[:, u % 2, c * BLK:(c + 1) * BLK]
                        mm(out, qeH[par][:, q], keep["kvTH"][:, keys], start=True, stop=False)
                        mm(out, qeH[par][:, q], keep["kvTL"][:, keys], start=False, stop=False)
                        last = mm(out, qeL[par][:, q], keep["kvTH"][:, keys], start=False, stop=True)
                    last.then_inc(scores_ready, 1)

                def pv(back, first, end):
                    batch = ((g - back) // NH if isinstance(g, int) else b) // 2
                    for n in range(first, end):
                        kt, src = n // 2, (PTH, PTL)[n % 2]
                        ins = mm(O[:], keep["kvn"][:, batch * KEYT + kt, :], src[par if back == 2 else 1 - par][:, kt, :],
                                 start=(n == 0), stop=(n == 2 * KEYT - 1))
                    if end == 2 * KEYT:
                        ins.then_inc(pv_done, 1)

                if on:
                    scores(0)
                if one:
                    pe.wait_ge(probs_ready, 4 * g - 1)
                    transposes(g, par, 2, 0, 0)
                if two:
                    pe.wait_ge(low_out, event(g - 1, 3))
                    pv(2, 8, 10)
                if one:
                    transposes(g, par, 2, 1, 1)
                if two:
                    pv(2, 10, 13)
                    pv(2, 13, 16)
                if on:
                    scores(1)
                if one:
                    pe.wait_ge(probs_ready, 4 * g)
                    transposes(g, par, 3, 2, 0)
                if two:
                    pe.wait_ge(wv_in[par], 16 * turns(g - 2, par))
                    pe.wait_ge(onorm_ready, g - 1)
                    mm(V[:], wv[par][:], onorm[:], start=False, stop=isinstance(h, int) and h == 1).then_inc(wv_done, 1)
                if one:
                    transposes(g, par, 3, 3, 1)
                if on:
                    scores(2)
                    pe.wait_ge(probs_ready, 4 * g + 1)
                    transposes(g, par, 0, 4, 0)
                if one:
                    if not isinstance(g, int) or g >= 2:
                        pe.wait_ge(onorm_ready, g - 1)
                    pe.wait_ge(low_out, event(g, 2))
                    pv(1, 0, 2)
                if on:
                    transposes(g, par, 0, 5, 1)
                if one:
                    pv(1, 2, 4)
                if exists(g + 1) and on:
                    project_queries(g, par)
                if on:
                    scores(3)
                    pe.wait_ge(probs_ready, 4 * g + 2)
                    transposes(g, par, 1, 7, 0)
                if one:
                    pv(1, 4, 6)
                if on:
                    transposes(g, par, 1, 8, 1)
                if one:
                    pv(1, 6, 8)
                if isinstance(h, int) and h == 1 and on:
                    if b:
                        pe.wait_ge(vsum_out, b)
                    else:
                        pe.wait_ge(bv_in, 16)
                        pe.wait_ge(ones_set, 1)
                    mm(V[:], bv[:], ones[:], start=True, stop=False)

            steps(pe, body)

        @block.scalar
        def _(act):
            def high(g, k, par, u, part, p):
                act.wait_ge(x_filled, event(g, k))
                nc.scalar.activation(PTH[p][:, 4 * part:4 * part + 4, u * P:(u + 1) * P],
                                     X[:, bank(g, k, par), :].rearrange("p (k c) -> p k c", k=4), ACT.Copy).then_inc(high_out, 1)

            def high_q(g, h, par):
                act.wait_ge(x_filled, event(g, 6))
                nc.scalar.activation(qeH[1 - par][:], X[:, bank(g, 6, par), :], ACT.Identity,
                                     bias=keep["beff"][:, ds(h, 1)]).then_inc(high_out, 1)

            high_q(-1, 0, 1)

            def body(g, b, h, par):
                on, one = exists(g), exists(g - 1)

                def exp(u):
                    col = par * UN + u
                    act.wait_ge(shift_ready, 4 * g + u + 1)
                    nc.scalar.activation(prob[u][:], S[:, u % 2, :], ACT.Exp, bias=shift[:, col:col + 1],
                                         accum_out=rs[:, col:col + 1]).then_inc(probs_ready, 1)

                for u in range(2):
                    if one:
                        high(g, 2 * u, par, 2 + u, 0, 1 - par)
                        high(g, 2 * u + 1, par, 2 + u, 1, 1 - par)
                    if on:
                        exp(u)
                if on:
                    if not isinstance(g, int) or g >= 2:
                        act.wait_ge(pv_done, g - 1)
                    high(g, 4, par, 0, 0, par)
                    high(g, 5, par, 0, 1, par)
                    exp(2)
                    if exists(g + 1):
                        high_q(g, h + 1 if not isinstance(g, int) else (h + 1) % NH, par)
                    high(g, 7, par, 1, 0, par)
                    high(g, 8, par, 1, 1, par)
                    exp(3)

            steps(act, body)

        @block.vector
        def _(dve):
            v = nc.vector

            def low(g, k, par, u, part, p):
                dve.wait_ge(high_out, event(g, k))
                at = (slice(None), slice(4 * part, 4 * part + 4), slice(u * P, (u + 1) * P))
                v.tensor_tensor(PTL[p][at], X[:, bank(g, k, par), :].rearrange("p (k c) -> p k c", k=4), f32(PTH[p][at]),
                                ALU.subtract).then_inc(low_out, 1)

            def low_q(g, h, par):
                dve.wait_ge(high_out, event(g, 6))
                v.scalar_tensor_tensor(out=qeL[1 - par][:], in0=X[:, bank(g, 6, par), :], scalar=keep["beff"][:, ds(h, 1)],
                                       in1=f32(qeH[1 - par][:]), op0=ALU.add, op1=ALU.subtract).then_inc(low_out, 1)

            low_q(-1, 0, 1)

            def body(g, b, h, par):
                on, one, two = exists(g), exists(g - 1), exists(g - 2)

                def maximum(u):
                    col = par * UN + u
                    dve.wait_ge(scores_ready, 4 * g + u + 1)
                    v.reduce_max(mx[:, col:col + 1], S[:, u % 2, :], AX.X).then_inc(max_ready, 1)

                def negated(u):
                    col = par * UN + u
                    bias = keep["c_all"][:, ds((b * NH + h) * UN + u, 1)]
                    dve.wait_ge(max_ready, 4 * g + u + 1)
                    v.scalar_tensor_tensor(out=shift[:, col:col + 1], in0=mx[:, col:col + 1], scalar=bias, in1=bias,
                                           op0=ALU.add, op1=ALU.subtract, reverse1=True).then_inc(shift_ready, 1)

                for u in range(2):
                    if u == 1 and two:
                        dve.wait_ge(pv_done, g - 1)
                        dve.wait_ge(row_in[par], 16 * turns(g - 2, par))
                        if not isinstance(g, int) or g >= 3:
                            dve.wait_ge(wv_done, g - 2)
                        v.tensor_tensor(onorm[:], O[:], recip_row[par][:], ALU.mult).then_inc(onorm_ready, 1)
                    if on:
                        maximum(u)
                    if one:
                        low(g, 2 * u, par, 2 + u, 0, 1 - par)
                    if on:
                        negated(u)
                    if one:
                        low(g, 2 * u + 1, par, 2 + u, 1, 1 - par)
                    if u == 0 and one:
                        dve.wait_ge(probs_ready, 4 * g)
                        if not isinstance(g, int) or g >= 3:
                            dve.wait_ge(recip_out, 16 * (g - 2))
                        v.reciprocal(recip[:, (1 - par) * UN:(2 - par) * UN],
                                     rs[:, (1 - par) * UN:(2 - par) * UN]).then_inc(recip_ready, 1)
                if isinstance(h, int) and h == 1 and b:
                    dve.wait_ge(wv_done, b * NH)
                    v.tensor_copy(keep["vsum"][:, (b - 1) * BLK:b * BLK], V[:]).then_inc(vsum_out, 1)
                if on:
                    for u in (2, 3):
                        k = 4 if u == 2 else 7
                        if u == 3 and exists(g + 1):
                            low_q(g, h + 1 if not isinstance(g, int) else (h + 1) % NH, par)
                        maximum(u)
                        low(g, k, par, u - 2, 0, par)
                        negated(u)
                        low(g, k + 1, par, u - 2, 1, par)

            steps(dve, body)


def feed_forward(nc, dram, keep):
    with ExitStack() as ctx:
        sb = lambda n, s, d=F32: ctx.enter_context(nc.sbuf_tensor(n, s, d))
        sem = lambda n: ctx.enter_context(nc.semaphore(n))
        kraw = sb("kraw", [P, 3, KT, HID], U8)
        w = sb("ffn_w", [P, 3, KT, HID], F32R)
        wo, bo = sb("wo", [P, HID]), sb("bo", [P, HID])
        sc, sc2 = sb("sc", [P, 3]), sb("sc2", [P, 3])
        row, row2 = sb("row", [P, KT]), sb("row2", [P, KT, 2])
        eps, spare = sb("eps4", [P, 1]), sb("spare", [P, 1])
        vs = sb("vs", [P, BLK])
        x1, y = sb("x1", [P, UN, HID]), sb("y", [P, UN, HID])
        xn2 = sb("xn2", [P, UN, HID])
        st, mv, std, rstd = sb("st4", [P, UN, 6]), sb("mv4", [P, UN, 2]), sb("std4", [P, UN]), sb("rstd4", [P, UN])
        aH = [sb(f"aH{i}", [P, KT, BLK], F32R) for i in range(2)]
        aL = [sb(f"aL{i}", [P, KT, BLK], F32R) for i in range(2)]
        hf = [sb(f"hf{i}", [P, BLK]) for i in range(2)]
        B = [ctx.enter_context(nc.psum_tensor(f"B{i}", [P, 512], F32)) for i in range(4)]
        names = ("c_in", "x4_in", "vs_ready", "mm_done", "const4", "w_ready", "biased", "summed", "stats", "std4_done",
                 "rstd4_done", "normed", "high_in", "split_in", "relu_done", "high_h", "split_h", "y_done", "stored")
        (c_in, x_in, vs_ready, mm_done, const, w_ready, biased, summed, stats, std_done, rstd_done, normed, high_in,
         split_in, relu_done, high_h, split_h, y_done, stored) = (sem(n) for n in names)
        ident = keep["ident"]
        MM = 20
        block = ctx.enter_context(nc.Block())

        @block.sync
        def _(sp):
            sp.dma_start(wo[:], dram["woT"]).then_inc(c_in, 16)
            sp.dma_start(bo[:], dram["bo"].partition_broadcast(P)).then_inc(c_in, 16)
            for j in range(3):
                sp.dma_start(kraw[:, j], dram[f"k{j}"].rearrange("(k p) n -> p k n", p=P)).then_inc(c_in, 16)
                sp.dma_start(sc[:, j:j + 1], dram[f"s{j}"].partition_broadcast(P)).then_inc(c_in, 16)
            with sp.Fori(0, NB) as n:
                sp.wait_ge(stored, 16 * n + 1)
                sp.dma_start(x1[:], dram["x"][ds(n * BLK, BLK), :].rearrange("(t p) d -> p t d", p=P)).then_inc(x_in, 16)
                sp.wait_ge(y_done, UN * n + UN + 1)
                sp.dma_start(dram["out"][ds(n * BLK, BLK), :].rearrange("(t p) d -> p t d", p=P), y[:]).then_inc(stored, 16)
            sp.wait_ge(stored, 16 * NB + 1)

        @block.gpsimd
        def _(pool):
            for free in (stored, y_done, mm_done):
                pool.sem_inc(free, 1)
            nc.gpsimd.memset(row[:], 1.0).then_inc(const, 1)
            nc.gpsimd.memset(eps[:], EPS).then_inc(const, 1)
            pool.wait_ge(const, 2)
            nc.gpsimd.affine_select(out=row[:], in_=row[:], compare_op=ALU.is_ge, fill=INH, base=EXC - 1,
                                    pattern=[[-P, KT]], channel_multiplier=-1).then_inc(const, 1)

        @block.tensor
        def _(pe):
            mm = nc.tensor.matmul
            pe.wait_ge(c_in, 128)
            with pe.Fori(0, NB) as n:
                pe.wait_ge(vs_ready, n + 1)
                pe.wait_ge(y_done, UN * n + 1)
                for t in range(UN):
                    mm(B[t][:], vs[:, t * P:(t + 1) * P], wo[:], start=True, stop=True).then_inc(mm_done, 1)
                pe.wait_ge(normed, UN * n + UN)
                for k in range(KT):
                    for t in range(UN):
                        last = nc.tensor.transpose(B[k][:, t * P:(t + 1) * P], xn2[:, t, k * P:(k + 1) * P], ident[:])
                    last.then_inc(mm_done, 1)
                pe.wait_ge(w_ready, 1)
                pe.wait_ge(split_in, KT * n + KT)
                for layer in range(2):
                    if layer:
                        pe.wait_ge(split_h, 2 * KT * n + KT)
                    for m in range(KT):
                        cols = slice(m * P, (m + 1) * P)
                        for k in range(KT):
                            mm(B[m][:], w[:, layer, k, cols], aH[layer][:, k, :], start=(k == 0), stop=False)
                            last = mm(B[m][:], w[:, layer, k, cols], aL[layer][:, k, :], start=False, stop=(k == KT - 1))
                        last.then_inc(mm_done, 1)
                pe.wait_ge(split_h, 2 * KT * n + 2 * KT)
                for t in range(UN):
                    tok = slice(t * P, (t + 1) * P)
                    for k in range(KT):
                        mm(B[t][:], aH[0][:, k, tok], w[:, 2, k, :], start=(k == 0), stop=False)
                        last = mm(B[t][:], aL[0][:, k, tok], w[:, 2, k, :], start=False, stop=(k == KT - 1))
                    last.then_inc(mm_done, 1)

        @block.scalar
        def _(act):
            act.wait_ge(const, 4)
            with act.Fori(0, NB) as n:
                act.wait_ge(mm_done, 1 + MM * n)
                nc.scalar.activation(vs[:], keep["vsum"][:, ds(n * BLK, BLK)], ACT.Copy).then_inc(vs_ready, 1)
                act.wait_ge(stats, 2 * UN * n + 2 * UN)
                nc.scalar.activation(std[:], mv[:, :, 1], ACT.Sqrt, bias=eps[:]).then_inc(std_done, 1)
                for k in range(KT):
                    act.wait_ge(mm_done, 1 + MM * n + UN + k + 1)
                    nc.scalar.activation(aH[0][:, k, :], B[k][:], ACT.Copy).then_inc(high_in, 1)
                for i in range(2 * KT):
                    layer, m = divmod(i, KT)
                    act.wait_ge(mm_done, 1 + MM * n + 8 + i + 1)
                    if i >= 2:
                        act.wait_ge(split_h, 2 * KT * n + i - 1)
                    nc.scalar.activation(hf[m % 2][:], B[m][:], ACT.Relu, scale=sc2[:, layer:layer + 1]).then_inc(relu_done, 1)

        @block.vector
        def _(dve):
            v = nc.vector
            dve.wait_ge(c_in, 128)
            dve.wait_ge(const, 3)
            v.tensor_scalar(sc2[:], sc[:], 2.0, None, ALU.mult)
            v.tensor_scalar(row2[:, :, 0], row[:], 2.0, None, ALU.mult)
            v.tensor_scalar(row2[:, :, 1], row[:], -1.0, None, ALU.mult).then_inc(const, 1)
            dve.wait_ge(const, 4)
            v.tensor_scalar(w[:, 0], kraw[:, 0], 2.0, -1.0, ALU.mult, ALU.add)
            for j in (1, 2):
                for k in range(KT):
                    last = v.tensor_scalar(w[:, j, k, :], kraw[:, j, k, :], row2[:, k, 0:1], row2[:, k, 1:2], ALU.mult, ALU.add)
            last.then_inc(w_ready, 1)
            with dve.Fori(0, NB) as n:
                dve.wait_ge(x_in, 16 * n + 16)
                for t in range(UN):
                    dve.wait_ge(mm_done, 1 + MM * n + t + 1)
                    v.tensor_tensor(y[:, t, :], B[t][:], bo[:], ALU.add).then_inc(biased, 1)
                dve.wait_ge(biased, UN * n + UN)
                v.tensor_tensor(x1[:], x1[:], y[:], ALU.add).then_inc(summed, 1)
                dve.wait_ge(summed, n + 1)
                for t in range(UN):
                    v.bn_stats(st[:, t, :], x1[:, t, :]).then_inc(stats, 1)
                dve.wait_ge(stats, 2 * UN * n + UN)
                v.memset(spare[:], 0.0)
                for t in range(UN):
                    v.bn_aggr(mv[:, t, :], st[:, t, :]).then_inc(stats, 1)
                dve.wait_ge(std_done, n + 1)
                v.reciprocal(rstd[:], std[:]).then_inc(rstd_done, 1)
                dve.wait_ge(rstd_done, n + 1)
                for t in range(UN):
                    v.tensor_scalar(xn2[:, t, :], x1[:, t, :], mv[:, t, 0:1], rstd[:, t:t + 1], ALU.subtract,
                                    ALU.mult).then_inc(normed, 1)
                for k in range(KT):
                    dve.wait_ge(high_in, KT * n + k + 1)
                    v.tensor_tensor(aL[0][:, k, :], B[k][:], f32(aH[0][:, k, :]), ALU.subtract).then_inc(split_in, 1)
                for i in range(2 * KT):
                    layer, m = divmod(i, KT)
                    to = 1 - layer
                    dve.wait_ge(relu_done, 2 * KT * n + i + 1)
                    v.tensor_copy(aH[to][:, m, :], hf[m % 2][:]).then_inc(high_h, 1)
                    dve.wait_ge(high_h, 2 * KT * n + i + 1)
                    v.tensor_tensor(aL[to][:, m, :], hf[m % 2][:], f32(aH[to][:, m, :]), ALU.subtract).then_inc(split_h, 1)
                for t in range(UN):
                    dve.wait_ge(mm_done, 1 + MM * n + 16 + t + 1)
                    v.scalar_tensor_tensor(out=y[:, t, :], in0=B[t][:], scalar=sc[:, 2:3], in1=x1[:, t, :],
                                           op0=ALU.mult, op1=ALU.add).then_inc(y_done, 1)


def layer(nc, dram):
    with ExitStack() as ctx:
        sb = lambda n, s, d=F32: ctx.enter_context(nc.sbuf_tensor(n, s, d))
        keep = {
            "ident": sb("ident", [P, P]), "beff": sb("beff", [P, NH]), "c_all": sb("c_all", [P, NG * UN]),
            "kvTH": sb("kvTH", [P, TOK], F32R), "kvTL": sb("kvTL", [P, TOK], F32R),
            "kvn": sb("kvn", [P, TT, P], F32R),
            "qaH": sb("qaH", [P, TOK], F32R), "qaL": sb("qaL", [P, TOK], F32R),
            "qbH": sb("qbH", [P, TOK], F32R), "qbL": sb("qbL", [P, TOK], F32R),
            "vsum": sb("vsum", [P, TOK]),
        }
        prepare(nc, dram, keep)
        attention(nc, dram, keep)
        feed_forward(nc, dram, keep)


def laid_out(a):
    t = lambda n: np.asarray(a["L0_attn_" + n])
    wq = t("Wq_up").reshape(NH, QHEAD, QL)
    bq = t("bq_up").reshape(NH, QHEAD)
    wkv = t("Wkv_up").reshape(NH, NOPE + VH, KVL)
    bkv = t("bkv_up").reshape(NH, NOPE + VH)
    twice = np.r_[0:P, P:QL, P:QL]
    raw = np.concatenate([wq[:, :NOPE][:, :, twice], wkv[:, :NOPE], bkv[:, :NOPE, None], bq[:, :NOPE, None],
                          wq[:, NOPE:].transpose(0, 2, 1)[:, 0:P],
                          wq[:, NOPE:].transpose(0, 2, 1)[:, np.r_[P:QL, P:QL]]], axis=2)
    wvT = wkv[:, NOPE:].transpose(0, 2, 1)
    bqc = t("bq_c")
    out = {
        "x": t("hidden_size").reshape(TOK, HID),
        "raw": raw.reshape(NH // HG, HG, P, R_N).transpose(0, 2, 1, 3).reshape(NH // HG, P, HG * R_N),
        "bqrT": bq[:, NOPE:].T,
        "wqcT": t("Wq_c").T[:, twice], "wkvcT": t("Wkv_c").T,
        "pb": np.stack([t("bkv_c"), bqc[:P], bqc[np.r_[P:QL, P:QL]]], axis=1),
        "wv": np.concatenate([wvT, wvT], axis=1), "bv": bkv[:, NOPE:],
        "woT": t("Wo").T, "bo": t("bo"),
    }
    for j in range(3):
        out[f"k{j}"] = np.asarray(a[f"L0_ffn_k{j}"])
        out[f"s{j}"] = np.asarray(a[f"L0_ffn_s{j}"]).reshape(1)
    return {n: np.ascontiguousarray(v) for n, v in out.items()}


def kernel(**inputs):
    import concourse.bacc as bacc
    from concourse.bass_utils import run_bass_kernel_spmd

    nc = bacc.Bacc("TRN2", target_bir_lowering=False, num_devices=1)
    arrays = laid_out(inputs)
    dram = {n: nc.dram_tensor("in_" + n, v.shape, mybir.dt.from_np(v.dtype), kind="ExternalInput").ap()
            for n, v in arrays.items()}
    dram["out"] = nc.dram_tensor("out", (TOK, HID), F32, kind="ExternalOutput").ap()
    dram["weff"] = nc.dram_tensor("weff_scratch", (NH // HG, HG, P, 3 * P), F32, kind="Internal").ap()
    dram["weff_h"] = dram["weff"].rearrange("g h p c -> (g h) p c")
    dram["row"] = nc.dram_tensor("row_scratch", (2, BLK), F32, kind="Internal").ap()
    layer(nc, dram)
    r = run_bass_kernel_spmd(nc, [{"in_" + n: v for n, v in arrays.items()}], core_ids=[0])
    return r.results[0]["out"].reshape(BATCH, SEQ, HID)
```

```python
from contextlib import ExitStack

import numpy as np
import concourse.bass as bass
from concourse import mybir

F32 = mybir.dt.float32
F32R = mybir.dt.float32r
U8 = mybir.dt.uint8
ACT = mybir.ActivationFunctionType
ALU = mybir.AluOpType
AX = mybir.AxisListType
ds = bass.ds

P = 128
NH = 32
NOPE, ROPE, VH = 128, 64, 128
QHEAD = NOPE + ROPE
QL, KVL = 192, 64
QB = QL - P
HID = 512
KT = HID // P
BATCH, SEQ = 2, 1024
TOK = BATCH * SEQ
TT = TOK // P
BLK = 512
NB = TOK // BLK
UN = BLK // P
KEYT = SEQ // P
NG = NB * NH
EPS = 1e-5
SCALE = float(1.0 / np.sqrt(QHEAD))
EXC = round(HID * 0.8)
INH = float(np.float32(-0.8 / (1.0 - 0.8)))
R_WK = QL
R_BK = R_WK + KVL
R_BQ = R_BK + 1
R_QR = R_BQ + 1
R_N = R_QR + 2 * ROPE
HG = 4


def f32(ap):
    return ap.bitcast(F32)


def prepare(nc, dram, keep):
    with ExitStack() as ctx:
        sb = lambda n, s, d=F32: ctx.enter_context(nc.sbuf_tensor(n, s, d))
        ps = lambda n: ctx.enter_context(nc.psum_tensor(n, [P, 512], F32))
        sem = lambda n: ctx.enter_context(nc.semaphore(n))
        raw = [sb(f"raw{i}", [P, HG, R_N]) for i in range(2)]
        full = sb("w_full", [P, HG, 2, P])
        split = [sb(f"w_split{i}", [P, HG, 3, P], F32R) for i in range(2)]
        wcA, wcB, bqk, bqr = (sb(n, [P, NH]) for n in ("wcA", "wcB", "bqk", "bqr"))
        wcAH, wcAL, wcBHL = (sb(n, [P, NH], F32R) for n in ("wcAH", "wcAL", "wcBHL"))
        scales = sb("scales", [P, HG, 2, ROPE])
        x_all = sb("x_all", [P, TT, HID])
        xn, xnH, xnL = keep["x0"], keep["w0"], sb("xnL", [P, KT, BLK], F32R)
        cT = xn[0:NH].rearrange("p t d -> p (t d)")
        wl = sb("w_latent", [P, KT, 3 * P])
        wlH, wlL = sb("w_latentH", [P, KT, 3 * P], F32R), sb("w_latentL", [P, KT, 3 * P], F32R)
        pb = sb("proj_bias", [P, 3])
        st, mv = sb("st", [P, UN, 6]), sb("mv", [P, UN, 2])
        std, rstd = sb("std", [P, UN]), sb("rstd", [P, UN])
        eps, ones, spare, bsum = (sb(n, [P, 1]) for n in ("eps", "ones", "spare_p", "bqk_sum"))
        kvf, qaf, qbf = sb("kvf", [P, BLK]), sb("qaf", [P, BLK]), sb("qbf", [P, BLK])
        psA, psB, psC = ps("psA"), ps("psB"), ps("psC")
        psT = [ps("psT0"), ps("psT1")]
        psN = ps("psN")
        psE, psF = ps("psE"), ps("psF")
        raw_in = [sem(f"raw_in{i}") for i in range(2)]
        split_out = [sem(f"split_out{i}") for i in range(2)]
        x_half = sem("x_half")
        bias_in, w_in, x_in, absorbed, emptied, rope_done, half_done, split_done, const = (
            sem(n) for n in ("bias_in", "w_in", "x_in", "absorbed", "emptied", "rope_done", "half_done", "split_done", "const"))
        stats, std_done, rstd_done, xn_ready, xn_used, xnH_ready, xnL_ready, wlH_ready, wlL_ready = (
            sem(n) for n in ("stats_p", "std_done", "rstd_done", "xn_ready", "xn_used", "xnH_ready", "xnL_ready",
                             "wlH_ready", "wlL_ready"))
        proj_done, proj_out, latent_low, n_done, n_high, n_out = (
            sem(n) for n in ("proj_done", "proj_out", "latent_low", "n_done", "n_high", "n_out"))
        wc_high, wc_ready, bsum_done, bsum_out, cT_done, cT_out, c_done = (
            sem(n) for n in ("wc_high", "wc_ready", "bsum_done", "bsum_out", "cT_done", "cT_out", "c_done"))
        groups = NH // HG
        W = 66
        vA = psE[:, 0:HG * W].rearrange("p (h c) -> p h c", c=W)
        vB = psF[:, 0:HG * W].rearrange("p (h c) -> p h c", c=W)
        ident = keep["ident"]
        block = ctx.enter_context(nc.Block())

        def turns(eng, head, turn):
            head(0)
            with eng.Fori(0, NB - 1) as n:
                turn(n, n + 1)
            turn(NB - 1, None)

        @block.gpsimd
        def _(pool):
            for free in (emptied, proj_out, latent_low, n_out, split_done, xn_used, xnL_ready, xnL_ready, *split_out):
                pool.sem_inc(free, 1)
            nc.gpsimd.memset(ident[:], 0.0).then_inc(const, 1)
            nc.gpsimd.memset(ones[:], 1.0).then_inc(const, 1)
            nc.gpsimd.memset(eps[:], EPS).then_inc(const, 1)
            nc.gpsimd.memset(scales[:], SCALE).then_inc(const, 1)
            pool.wait_ge(const, 4)
            nc.gpsimd.affine_select(out=ident[:], in_=ident[:], compare_op=ALU.not_equal, fill=1.0, base=0,
                                    pattern=[[-1, P]], channel_multiplier=1).then_inc(const, 1)
            pool.wait_ge(wlH_ready, 1)
            nc.gpsimd.tensor_tensor(wlL[:], wl[:], f32(wlH[:]), ALU.subtract).then_inc(wlL_ready, 1)

            def scale_rope(n, i):
                pool.wait_ge(raw_in[i], 16 * n + 16)
                pool.wait_ge(split_done, 2 * n + i + 1)
                nc.gpsimd.tensor_tensor(full[:, :, :, KVL:P], raw[i][:, :, R_QR:R_N].rearrange("p h (s c) -> p h s c", s=2),
                                        scales[:], ALU.mult).then_inc(rope_done, 1)

            def low_latents(n, which):
                tok = ds(n * BLK, BLK)
                for j in which:
                    src, rows, part = ((kvf, P, "kvT"), (qaf, P, "qa"), (qbf, QB, "qb"))[j]
                    pool.wait_ge(proj_out, 3 * n + j + 2)
                    nc.gpsimd.tensor_tensor(keep[part + "L"][0:rows, tok], src[0:rows, :], f32(keep[part + "H"][0:rows, tok]),
                                            ALU.subtract).then_inc(latent_low, 1)

            with pool.Fori(0, NB - 1) as n:
                scale_rope(n, 0)
                low_latents(n, range(3))
                scale_rope(n, 1)
            scale_rope(NB - 1, 0)
            low_latents(NB - 1, (0,))
            scale_rope(NB - 1, 1)
            low_latents(NB - 1, (1, 2))

        @block.sync
        def _(sp):
            def load(g, i):
                sp.dma_start(raw[i][:], dram["raw"][g].rearrange("p (h c) -> p h c", h=HG)).then_inc(raw_in[i], 16)

            def load_x(n):
                sp.wait_ge(x_in, 16 * n)
                sp.dma_start(x_all[:, UN * n:UN * (n + 1), :],
                             dram["x"][n * BLK:(n + 1) * BLK, :].rearrange("(t p) d -> p t d", p=P)).then_inc(x_in, 16)

            def store(g, i):
                sp.dma_start(dram["weff"][g].rearrange("h p c -> p h c"),
                             f32(split[i][:].rearrange("p h t c -> p h (t c)"))).then_inc(split_out[i], 16)

            for half, loaded in enumerate((x_half, x_in)):
                sp.dma_start(x_all[:, 2 * half:2 * half + 2, :],
                             dram["x"][2 * half * P:2 * (half + 1) * P, :].rearrange("(t p) d -> p t d", p=P)).then_inc(loaded, 16)
            sp.dma_start(wl[:], dram["wlT"].rearrange("(k p) c -> p k c", p=P)).then_inc(w_in, 16)
            sp.dma_start(pb[:], dram["pb"]).then_inc(w_in, 16)
            load_x(1)
            load(0, 0)
            load(1, 1)
            sp.dma_start(bqr[P - ROPE:P, :], dram["bqrT"]).then_inc(bias_in, 16)
            load_x(2)
            load_x(3)
            with sp.Fori(0, groups // 2 - 1) as g2:
                for i in range(2):
                    sp.wait_ge(half_done, 4 * g2 + 2 * i + 1)
                    load(2 * g2 + i + 2, i)
                    sp.wait_ge(split_done, 2 * g2 + i + 2)
                    store(2 * g2 + i, i)
            for i in range(2):
                sp.wait_ge(split_done, groups + i)
                store(groups - 2 + i, i)
            for i in range(2):
                sp.wait_ge(split_out[i], 16 * (groups // 2) + 1)
            for i in range(2):
                sp.dma_start(f32(keep["weff"][i][:].rearrange("p t c -> p (t c)")),
                             dram["weff_h"][i]).then_inc(keep["weff_in"][i], 16)

        @block.tensor
        def _(pe):
            mm = nc.tensor.matmul

            def turned(n, tiles):
                for t in tiles:
                    pe.wait_ge(xnL_ready, UN * n + t + 1)
                    pe.wait_ge(xn_ready, UN * n + t + 1)
                    for k in range(KT):
                        last = nc.tensor.transpose(psT[t % 2][:, k * P:(k + 1) * P], xn[:, t, k * P:(k + 1) * P], ident[:])
                    last.then_inc(xn_used, 1)

            def project(n, which):
                if 0 in which:
                    pe.wait_ge(xnL_ready, UN * n + UN + 2)
                    pe.wait_ge(proj_out, 3 * n + 1)
                for j in which:
                    out, c = (psA, psB, psC)[j], slice(j * P, (j + 1) * P)
                    for k in range(KT):
                        mm(out[:], wlH[:, k, c], xnH[:, k, :], start=(k == 0), stop=False)
                        mm(out[:], wlH[:, k, c], xnL[:, k, :], start=False, stop=False)
                        last = mm(out[:], wlL[:, k, c], xnH[:, k, :], start=False, stop=(k == KT - 1))
                    last.then_inc(proj_done, 1)

            def absorb(n, i):
                pe.wait_ge(raw_in[i], 16 * n + 16)
                pe.wait_ge(emptied, 2 * n + i + 1)
                for h in range(HG):
                    right = raw[i][:, h, R_WK:R_WK + W]
                    mm(vA[:, h, :], raw[i][:, h, 0:P], right, start=True, stop=True)
                    last = mm(vB[:, h, :], raw[i][:, h, P:R_BK], right, start=True, stop=True)
                last.then_inc(absorbed, 1)

            def head(n):
                pe.wait_ge(const, 5)
                turned(n, range(UN))
                pe.wait_ge(wlL_ready, 1)

            def turn_back(n):
                for u in range(UN):
                    last = nc.tensor.transpose(psN[:, u * KVL:(u + 1) * KVL], kvf[0:KVL, u * P:(u + 1) * P],
                                               ident[0:KVL, 0:KVL])
                last.then_inc(n_done, 1)

            def turn(n, nxt):
                if nxt is None:
                    project(n, (0,))
                    absorb(n, 0)
                    project(n, (1,))
                    absorb(n, 1)
                    project(n, (2,))
                else:
                    project(n, range(3))
                    turned(nxt, (0, 1))
                    absorb(n, 0)
                pe.wait_ge(n_out, n + 1)
                pe.wait_ge(proj_out, 3 * n + 2)
                if nxt is not None:
                    turned(nxt, (2, 3))
                turn_back(n)
                if nxt is not None:
                    absorb(n, 1)

            turns(pe, head, turn)
            pe.wait_ge(wc_ready, 1)
            mm(psA[0:NH, 0:1], bqk[:], ones[:], start=True, stop=True).then_inc(bsum_done, 1)
            banks = (psT[0], psT[1], psE, psF)
            for n in range(NB):
                tok, out = slice(n * BLK, (n + 1) * BLK), banks[n][0:NH, :]
                pe.wait_ge(latent_low, 3 * n + 4)
                mm(out, wcAH[:], keep["qaH"][:, tok], start=True, stop=False)
                mm(out, wcAH[:], keep["qaL"][:, tok], start=False, stop=False)
                mm(out, wcAL[:], keep["qaH"][:, tok], start=False, stop=False)
                mm(out, wcBHL[:], keep["qbH"][:, tok], start=False, stop=False)
                mm(out, wcBHL[0:QB, :], keep["qbL"][0:QB, tok], start=False, stop=True).then_inc(cT_done, 1)
            for n in range(NB):
                pe.wait_ge(cT_out, n + 1)
                for t in range(UN * n, UN * (n + 1)):
                    last = nc.tensor.transpose(psA[:, t * NH:(t + 1) * NH], cT[:, t * P:(t + 1) * P], ident[0:NH, 0:NH])
            last.then_inc(c_done, 1)

        @block.scalar
        def _(act):
            def deviation(n):
                act.wait_ge(stats, 2 * UN * n + 2 * UN)
                nc.scalar.activation(std[:], mv[:, :, 1], ACT.Sqrt, bias=eps[:]).then_inc(std_done, 1)

            def read_turned(n, tiles):
                for t in tiles:
                    act.wait_ge(xn_used, UN * n + t + 2)
                    nc.scalar.activation(xnH[:, :, t * P:(t + 1) * P], psT[t % 2][:].rearrange("p (k c) -> p k c", k=KT),
                                         ACT.Copy).then_inc(xnH_ready, 1)

            def read_absorbed(n, i):
                g = 2 * n + i
                act.wait_ge(absorbed, g + 1)
                act.wait_ge(split_done, g + 1)
                heads = ds(g * HG, HG)
                nc.scalar.activation(full[:, :, 0, 0:KVL], vA[:, :, 0:KVL], ACT.Copy, scale=SCALE)
                nc.scalar.activation(full[0:QB, :, 1, 0:KVL], vB[0:QB, :, 0:KVL], ACT.Copy, scale=SCALE)
                nc.scalar.activation(wcA[:, heads], vA[:, :, KVL], ACT.Copy, scale=SCALE)
                nc.scalar.activation(wcB[0:QB, heads], vB[0:QB, :, KVL], ACT.Copy, scale=SCALE)
                nc.scalar.activation(keep["beff"][0:KVL, heads], vB[QB:P, :, KVL + 1], ACT.Copy,
                                     scale=SCALE).then_inc(emptied, 1)

            def head(n):
                act.wait_ge(const, 4)
                deviation(n)
                act.wait_ge(w_in, 32)
                nc.scalar.activation(wlH[:], wl[:], ACT.Copy).then_inc(wlH_ready, 1)
                read_turned(n, range(UN))

            def read_projected(n, which):
                tok = ds(n * BLK, BLK)
                for j in which:
                    out, src, hi = ((kvf, psA, "kvTH"), (qaf, psB, "qaH"), (qbf, psC, "qbH"))[j]
                    act.wait_ge(proj_done, 3 * n + j + 1)
                    nc.scalar.activation(out[:], src[:], ACT.Identity, bias=pb[:, j:j + 1])
                    nc.scalar.activation(keep[hi][:, tok], src[:], ACT.Identity, bias=pb[:, j:j + 1]).then_inc(proj_out, 1)

            def turn(n, nxt):
                if nxt is not None:
                    deviation(nxt)
                act.wait_ge(n_out, n + 1)
                act.wait_ge(latent_low, 3 * n + 1)
                if nxt is not None:
                    read_projected(n, range(3))
                    read_turned(nxt, (0, 1))
                    read_absorbed(n, 0)
                    read_turned(nxt, (2, 3))
                    read_absorbed(n, 1)
                else:
                    read_projected(n, (0,))
                    read_absorbed(n, 0)
                    read_projected(n, (1,))
                    read_absorbed(n, 1)
                    read_projected(n, (2,))

            turns(act, head, turn)
            act.wait_ge(bsum_done, 1)
            nc.scalar.activation(bsum[0:NH, :], psA[0:NH, 0:1], ACT.Copy).then_inc(bsum_out, 1)
            act.wait_ge(bsum_out, 1)
            for n, out in enumerate((psT[0], psT[1], psE, psF)):
                act.wait_ge(cT_done, n + 1)
                nc.scalar.activation(cT[:, n * BLK:(n + 1) * BLK], out[0:NH, :], ACT.Identity,
                                     bias=bsum[0:NH, :]).then_inc(cT_out, 1)

        @block.vector
        def _(dve):
            v = nc.vector

            def norm(n):
                rows = lambda t: x_all[:, ds(UN * n + t, 1), :].rearrange("p o d -> p (o d)")
                dve.wait_ge(x_half if isinstance(n, int) else x_in, 16 * n + 16)
                v.memset(spare[:], 0.0)
                for t in range(UN):
                    if t == 2 and isinstance(n, int):
                        dve.wait_ge(x_in, 16)
                    v.bn_stats(st[:, t, :], rows(t)).then_inc(stats, 1)
                dve.wait_ge(stats, 2 * UN * n + UN)
                v.memset(spare[:], 0.0)
                for t in range(UN):
                    v.bn_aggr(mv[:, t, :], st[:, t, :]).then_inc(stats, 1)
                dve.wait_ge(std_done, n + 1)
                v.reciprocal(rstd[:], std[:]).then_inc(rstd_done, 1)
                dve.wait_ge(rstd_done, n + 1)
                dve.wait_ge(xn_used, UN * n + 1)
                for t in range(UN):
                    v.tensor_scalar(xn[:, t, :], rows(t), mv[:, t, 0:1], rstd[:, t:t + 1],
                                    ALU.subtract, ALU.mult).then_inc(xn_ready, 1)

            def low_turned(n, tiles):
                for t in tiles:
                    dve.wait_ge(xnH_ready, UN * n + t + 1)
                    at = (slice(None), slice(None), slice(t * P, (t + 1) * P))
                    v.tensor_tensor(xnL[at], psT[t % 2][:].rearrange("p (k c) -> p k c", k=KT), f32(xnH[at]),
                                    ALU.subtract).then_inc(xnL_ready, 1)

            def split_absorbed(n, i):
                g = 2 * n + i
                heads = ds(g * HG, HG)
                dve.wait_ge(raw_in[i], 16 * n + 16)
                v.scalar_tensor_tensor(out=bqk[:, heads], in0=raw[i][:, :, R_BK], scalar=SCALE,
                                       in1=raw[i][:, :, R_BQ], op0=ALU.mult, op1=ALU.mult)
                dve.wait_ge(rope_done, g + 1)
                dve.wait_ge(emptied, g + 2)
                dve.wait_ge(split_out[i], 16 * n + 1)
                high, low = split[i][:, :, 0, :], split[i][:, :, 1, :]
                v.tensor_copy(high, full[:, :, 0, :]).then_inc(half_done, 1)
                v.tensor_copy(split[i][0:QB, :, 2, :], full[0:QB, :, 1, :]).then_inc(half_done, 1)
                dve.wait_ge(half_done, 2 * g + 1)
                v.tensor_tensor(low, full[:, :, 0, :], f32(high), ALU.subtract)
                dve.wait_ge(half_done, 2 * g + 2)
                v.tensor_tensor(split[i][QB:P, :, 2, :], full[0:QB, :, 1, :], f32(split[i][0:QB, :, 2, :]),
                                ALU.subtract).then_inc(split_done, 1)

            def head(n):
                norm(n)
                low_turned(n, range(UN))

            def turn(n, nxt):
                if nxt is not None:
                    norm(nxt)
                if nxt is not None:
                    low_turned(nxt, (0, 1))
                split_absorbed(n, 0)
                if nxt is not None:
                    low_turned(nxt, (2, 3))
                split_absorbed(n, 1)
                if nxt is None:
                    dve.wait_ge(emptied, groups + 1)
                    v.tensor_copy(wcAH[:], wcA[:]).then_inc(wc_high, 1)
                    v.tensor_copy(wcBHL[0:QB, :], wcB[0:QB, :]).then_inc(wc_high, 1)
                    dve.wait_ge(wc_high, 2)
                    v.tensor_tensor(wcAL[:], wcA[:], f32(wcAH[:]), ALU.subtract)
                    v.tensor_tensor(wcBHL[QB:P, :], wcB[0:QB, :], f32(wcBHL[0:QB, :]), ALU.subtract).then_inc(wc_ready, 1)
                dve.wait_ge(n_done, n + 1)
                four = psN[:, 0:UN * KVL].rearrange("p (u c) -> p u c", u=UN)
                kvn = keep["kvn"][:, ds(UN * n, UN), :]
                v.tensor_copy(kvn[:, :, 0:KVL], four).then_inc(n_high, 1)
                dve.wait_ge(n_high, n + 1)
                v.tensor_tensor(kvn[:, :, KVL:P], four, f32(kvn[:, :, 0:KVL]), ALU.subtract).then_inc(n_out, 1)

            turns(dve, head, turn)
            dve.wait_ge(bias_in, 16)
            v.tensor_scalar(keep["beff"][KVL:P, :], bqr[KVL:P, :], SCALE, None, ALU.mult)
            dve.wait_ge(c_done, 1)
            v.tensor_copy(keep["c_all"][:].rearrange("p (n h u) -> p n u h", n=NB, h=NH),
                          psA[:].rearrange("p (n u h) -> p n u h", n=NB, h=NH))


def event(g, k):
    if isinstance(g, int):
        if g == -1:
            return 1
        if g == NG or (g == NG - 1 and k > 6):
            return 9 * g + k - 3
    return 9 * g + k - 2


def bank(g, k, par):
    return event(g, k) % 2 if isinstance(g, int) else (par + k) % 2


def attention(nc, dram, keep):
    with ExitStack() as ctx:
        sb = lambda n, s, d=F32: ctx.enter_context(nc.sbuf_tensor(n, s, d))
        sem = lambda n: ctx.enter_context(nc.semaphore(n))
        weff, weff_in = keep["weff"], keep["weff_in"]
        wv = [sb(f"wv{i}", [P, VH]) for i in range(2)]
        wvH = [sb(f"wvH{i}", [P, VH], F32R) for i in range(2)]
        wvHL = [sb(f"wvHL{i}", [P, VH], F32R) for i in range(2)]
        qeH = [sb(f"qeH{i}", [P, BLK], F32R) for i in range(2)]
        qeL = [sb(f"qeL{i}", [P, BLK], F32R) for i in range(2)]
        prob = [sb(f"prob{i}", [P, SEQ]) for i in range(UN)]
        PTH = [sb(f"PTH{i}", [P, KEYT, BLK], F32R) for i in range(2)]
        PTL = [sb(f"PTL{i}", [P, KEYT, BLK], F32R) for i in range(2)]
        onorm, onormH, onormLH = sb("onorm", [P, BLK]), sb("onormH", [P, BLK], F32R), sb("onormLH", [P, BLK], F32R)
        recip_row = [sb(f"recip_row{i}", [P, BLK]) for i in range(2)]
        mx, shift, rs, recip = (sb(n, [P, 2 * UN]) for n in ("mx", "shift", "rs", "recip"))
        bv, ones = sb("bv", [NH, VH]), sb("ones_row", [NH, BLK])
        unit = sb("unit_tile", [P, VH])
        S = ctx.enter_context(nc.psum_tensor("S", [P, 2, SEQ], F32))
        X = ctx.enter_context(nc.psum_tensor("X", [P, 2, BLK], F32))
        O = ctx.enter_context(nc.psum_tensor("O", [P, BLK], F32))
        V = ctx.enter_context(nc.psum_tensor("V", [P, BLK], F32))
        wv_in = [sem(f"wv_in{i}") for i in range(2)]
        row_in = [sem(f"row_in{i}") for i in range(2)]
        names = ("bv_in", "ones_set", "scores_ready", "max_ready", "shift_ready", "probs_ready", "x_filled",
                 "high_out", "low_out", "recip_ready", "recip_out", "pv_done", "onorm_ready", "wv_done", "vsum_out",
                 "wv_split", "onorm_high", "onorm_low", "ffn_in", "row_ready", "bo_added", "projected0", "summed0",
                 "stats0", "std0_done")
        (bv_in, ones_set, scores_ready, max_ready, shift_ready, probs_ready, x_filled, high_out, low_out,
         recip_ready, recip_out, pv_done, onorm_ready, wv_done, vsum_out,
         wv_split, onorm_high, onorm_low, ffn_in, row_ready, bo_added, projected0, summed0,
         stats0, std0_done) = (sem(n) for n in names)
        ident = keep["ident"]
        projection = [S[:, t // 2, (t % 2) * BLK:(t % 2 + 1) * BLK] for t in range(UN)]
        block = ctx.enter_context(nc.Block())

        def steps(eng, body, after=2):
            for b in range(NB):
                for h in (0, 1):
                    body(b * NH + h, b, h, h)
                with eng.Fori(1, NH // 2 - 1) as pair:
                    for par in range(2):
                        body(b * NH + 2 * pair + par, b, 2 * pair + par, par)
                for h in (NH - 2, NH - 1):
                    body(b * NH + h, b, h, h % 2)
            for g in range(NG, NG + after):
                body(g, NB, g - NG, g % 2)

        def exists(g):
            return not isinstance(g, int) or 0 <= g < NG

        def turns(g, par):
            return g // 2 + 1 if isinstance(g, int) else (g - par) // 2 + 1

        @block.sync
        def _(sp):
            def load(g, weights, par):
                sp.wait_ge(x_filled, event(g - 3, 6))
                sp.dma_start(f32(weff[par][:].rearrange("p t c -> p (t c)")), weights).then_inc(weff_in[par], 16)

            two_on = dram["weff_h"][2:NH]
            sp.dma_start(bv[:], dram["bv"]).then_inc(bv_in, 16)
            sp.dma_start(keep["x0"][:], dram["x"][0:BLK, :].rearrange("(t p) d -> p t d", p=P)).then_inc(ffn_in, 16)
            sp.dma_start(keep["wo"][:], dram["woT"]).then_inc(ffn_in, 16)
            sp.dma_start(keep["bo"][:], dram["bo"].partition_broadcast(P)).then_inc(ffn_in, 16)
            for j in range(3):
                sp.dma_start(keep["flags"][:, j], dram[f"k{j}"].rearrange("(k p) n -> p k n", p=P)).then_inc(ffn_in, 16)
                sp.dma_start(keep["sc"][:, j:j + 1], dram[f"s{j}"].partition_broadcast(P)).then_inc(ffn_in, 16)

            def body(g, b, h, par):
                if exists(g - 1):
                    last = 1 - par
                    sp.wait_ge(recip_ready, g)
                    with nc.allow_non_contiguous_dma(reason="512 numbers, turned from columns into a row"):
                        sp.dma_start(dram["row"][last].rearrange("(u p) -> p u", p=P),
                                     recip[:, last * UN:(last + 1) * UN]).then_inc(recip_out, 16)
                    sp.wait_ge(recip_out, 16 * g)
                    sp.dma_start(recip_row[last][:], dram["row"][last].partition_broadcast(P)).then_inc(row_in[last], 16)
                if exists(g + 2):
                    load(g + 2, two_on[h] if not isinstance(g, int) else dram["weff_h"][(h + 2) % NH], par)

            steps(sp, body, after=1)

        @block.gpsimd
        def _(pool):
            copied = sem("wv_copied")
            nc.gpsimd.memset(ones[:], 1.0).then_inc(ones_set, 1)
            nc.gpsimd.memset(unit[:], 1.0).then_inc(ones_set, 1)
            pool.wait_ge(ones_set, 2)

            def ahead(b):
                row, row2 = keep["row"], keep["row2"]
                if b == 1:
                    nc.gpsimd.memset(keep["eps4"][:], EPS)
                    nc.gpsimd.memset(row[:], 1.0).then_inc(row_ready, 1)
                    pool.wait_ge(row_ready, 1)
                    nc.gpsimd.affine_select(out=row[:], in_=row[:], compare_op=ALU.is_ge, fill=INH, base=EXC - 1,
                                            pattern=[[-P, KT]], channel_multiplier=-1).then_inc(row_ready, 1)
                    pool.wait_ge(row_ready, 2)
                    nc.gpsimd.tensor_scalar(row2[:, :, 0], row[:], 2.0, None, ALU.mult)
                    nc.gpsimd.tensor_scalar(row2[:, :, 1], row[:], -1.0, None, ALU.mult)
                if b == 2:
                    pool.wait_ge(ffn_in, 16 * 9)
                    nc.gpsimd.tensor_scalar(keep["w0"][:], keep["flags"][:, 0], 2.0, -1.0, ALU.mult, ALU.add)
                if b == 3:
                    for t in range(UN):
                        last = nc.gpsimd.tensor_tensor(keep["x0"][:, t, :], keep["x0"][:, t, :], keep["bo"][:], ALU.add)
                    last.then_inc(bo_added, 1)

            def body(g, b, h, par):
                if isinstance(h, int) and h == 1 and 0 < b < NB:
                    pool.wait_ge(wv_split, g - 1)
                    pool.wait_ge(onorm_low, g - 2)
                    ahead(b)
                if exists(g):
                    if not isinstance(g, int) or g >= 2:
                        pool.wait_ge(wv_split, g - 1)
                    pool.dma_start(wv[par][:], dram["wv"][h]).then_inc(wv_in[par], 16)
                if exists(g - 1):
                    i = 1 - par
                    if not isinstance(g, int) or g >= 3:
                        pool.wait_ge(wv_done, g - 2)
                    pool.wait_ge(wv_in[i], 16 * turns(g - 1, i))
                    nc.gpsimd.tensor_tensor(wvH[i][:], wv[i][:], unit[:], ALU.mult).then_inc(copied, 1)
                    nc.gpsimd.tensor_tensor(wvHL[i][0:KVL, :], wv[i][0:KVL, :], unit[0:KVL, :], ALU.mult)
                    pool.wait_ge(copied, g)
                    nc.gpsimd.tensor_tensor(wvHL[i][KVL:P, :], wv[i][KVL:P, :], f32(wvH[i][KVL:P, :]),
                                            ALU.subtract).then_inc(wv_split, 1)
                if exists(g - 2):
                    pool.wait_ge(onorm_high, 2 * g - 3)
                    nc.gpsimd.tensor_tensor(onormLH[0:KVL, :], onorm[0:KVL, :], f32(onormH[0:KVL, :]),
                                            ALU.subtract).then_inc(onorm_low, 1)

            steps(pool, body)

        @block.tensor
        def _(pe):
            mm = nc.tensor.matmul

            def free_bank(g, k, par):
                if not isinstance(g, int) or event(g, k) > 2:
                    pe.wait_ge(low_out, event(g, k) - 2)
                return X[:, bank(g, k, par), :]

            def project_queries(g, par):
                out = free_bank(g, 6, par)
                nxt = g + 1
                pe.wait_ge(weff_in[1 - par], 16 * turns(nxt, 1 - par))
                b = nxt // NH if isinstance(g, int) else block_now[0]
                tok = slice(b * BLK, (b + 1) * BLK)
                w = weff[1 - par]
                mm(out, w[:, 0, :], keep["qaH"][:, tok], start=True, stop=False)
                mm(out, w[:, 0, :], keep["qaL"][:, tok], start=False, stop=False)
                mm(out, w[:, 1, :], keep["qaH"][:, tok], start=False, stop=False)
                mm(out, w[:, 2, :], keep["qbH"][:, tok], start=False, stop=False)
                mm(out, w[0:QB, 2, :], keep["qbL"][0:QB, tok], start=False, stop=True).then_inc(x_filled, 1)

            def transposes(g, par, unit, k, part):
                out = free_bank(g, k, par)
                for j in range(4):
                    last = nc.tensor.transpose(out[:, j * P:(j + 1) * P],
                                               prob[unit][:, (4 * part + j) * P:(4 * part + j + 1) * P], ident[:])
                last.then_inc(x_filled, 1)

            block_now = [0]
            project_queries(-1, 1)

            def body(g, b, h, par):
                block_now[0] = b
                on, one, two = exists(g), exists(g - 1), exists(g - 2)

                def scores(u):
                    if u == 0:
                        pe.wait_ge(low_out, event(g - 1, 6))
                    if not isinstance(g, int) or 4 * g + u >= 2:
                        pe.wait_ge(probs_ready, 4 * g + u - 1)
                    q = slice(u * P, (u + 1) * P)
                    for c in range(2):
                        keys = slice((b // 2) * SEQ + c * BLK, (b // 2) * SEQ + (c + 1) * BLK)
                        out = S[:, u % 2, c * BLK:(c + 1) * BLK]
                        mm(out, qeH[par][:, q], keep["kvTH"][:, keys], start=True, stop=False)
                        mm(out, qeH[par][:, q], keep["kvTL"][:, keys], start=False, stop=False)
                        last = mm(out, qeL[par][:, q], keep["kvTH"][:, keys], start=False, stop=True)
                    last.then_inc(scores_ready, 1)

                def pv(back, first, end):
                    batch = ((g - back) // NH if isinstance(g, int) else b) // 2
                    for n in range(first, end):
                        kt, src = n // 2, (PTH, PTL)[n % 2]
                        ins = mm(O[:], keep["kvn"][:, batch * KEYT + kt, :], src[par if back == 2 else 1 - par][:, kt, :],
                                 start=(n == 0), stop=(n == 2 * KEYT - 1))
                    if end == 2 * KEYT:
                        ins.then_inc(pv_done, 1)

                if on:
                    scores(0)
                if one:
                    pe.wait_ge(probs_ready, 4 * g - 1)
                    transposes(g, par, 2, 0, 0)
                if two:
                    pe.wait_ge(low_out, event(g - 1, 3))
                    pv(2, 8, 10)
                if one:
                    transposes(g, par, 2, 1, 1)
                if two:
                    pv(2, 10, 16)
                if on:
                    scores(1)
                if one:
                    pe.wait_ge(probs_ready, 4 * g)
                    transposes(g, par, 3, 2, 0)
                if one:
                    transposes(g, par, 3, 3, 1)
                if isinstance(g, int) and g == NG:
                    pe.wait_ge(vsum_out, 1)
                    pe.wait_ge(ffn_in, 16 * 9)
                    for t in range(UN):
                        mm(projection[t], keep["vsum"][:, t * P:(t + 1) * P], keep["wo"][:],
                           start=True, stop=True).then_inc(projected0, 1)
                if on:
                    scores(2)
                    pe.wait_ge(probs_ready, 4 * g + 1)
                    transposes(g, par, 0, 4, 0)
                if one:
                    if not isinstance(g, int) or g >= 2:
                        pe.wait_ge(onorm_ready, g - 1)
                    pe.wait_ge(low_out, event(g, 2))
                    pv(1, 0, 2)
                if on:
                    transposes(g, par, 0, 5, 1)
                if one:
                    pv(1, 2, 4)
                if one:
                    pv(1, 4, 8)
                if exists(g + 1) and on:
                    project_queries(g, par)
                if on:
                    scores(3)
                    pe.wait_ge(probs_ready, 4 * g + 2)
                    transposes(g, par, 1, 7, 0)
                if two:
                    pe.wait_ge(wv_split, g - 1)
                    pe.wait_ge(onorm_high, 2 * g - 2)
                    pe.wait_ge(onorm_low, g - 1)
                    mm(V[:], wvH[par][:], onormH[:], start=False, stop=False)
                    mm(V[:], wvHL[par][:], onormLH[:], start=False, stop=isinstance(h, int) and h == 1).then_inc(wv_done, 1)
                if on:
                    transposes(g, par, 1, 8, 1)
                if isinstance(h, int) and h == 1 and on:
                    if b:
                        pe.wait_ge(vsum_out, b)
                    else:
                        pe.wait_ge(bv_in, 16)
                        pe.wait_ge(ones_set, 1)
                    mm(V[:], bv[:], ones[:], start=True, stop=False)

            steps(pe, body)

        @block.scalar
        def _(act):
            def high(g, k, par, u, part, p):
                act.wait_ge(x_filled, event(g, k))
                nc.scalar.activation(PTH[p][:, 4 * part:4 * part + 4, u * P:(u + 1) * P],
                                     X[:, bank(g, k, par), :].rearrange("p (k c) -> p k c", k=4), ACT.Copy).then_inc(high_out, 1)

            def high_q(g, h, par):
                act.wait_ge(x_filled, event(g, 6))
                nc.scalar.activation(qeH[1 - par][:], X[:, bank(g, 6, par), :], ACT.Identity,
                                     bias=keep["beff"][:, ds(h, 1)]).then_inc(high_out, 1)

            high_q(-1, 0, 1)

            def body(g, b, h, par):
                on, one = exists(g), exists(g - 1)

                def exp(u):
                    col = par * UN + u
                    act.wait_ge(shift_ready, 4 * g + u + 1)
                    nc.scalar.activation(prob[u][:], S[:, u % 2, :], ACT.Exp, bias=shift[:, col:col + 1],
                                         accum_out=rs[:, col:col + 1]).then_inc(probs_ready, 1)

                for u in range(2):
                    if one:
                        high(g, 2 * u, par, 2 + u, 0, 1 - par)
                        high(g, 2 * u + 1, par, 2 + u, 1, 1 - par)
                    if u == 1 and exists(g - 2):
                        if not isinstance(g, int) or g >= 3:
                            act.wait_ge(wv_done, g - 2)
                        act.wait_ge(onorm_ready, g - 1)
                        nc.scalar.activation(onormH[:], onorm[:], ACT.Copy).then_inc(onorm_high, 1)
                    if on:
                        exp(u)
                if on:
                    if not isinstance(g, int) or g >= 2:
                        act.wait_ge(pv_done, g - 1)
                    high(g, 4, par, 0, 0, par)
                    high(g, 5, par, 0, 1, par)
                if exists(g - 2):
                    nc.scalar.activation(onormLH[KVL:P, :], onorm[0:KVL, :], ACT.Copy).then_inc(onorm_high, 1)
                if isinstance(g, int) and g == NG + 1:
                    act.wait_ge(row_ready, 1)
                    act.wait_ge(stats0, 2 * UN)
                    nc.scalar.activation(keep["std0"][:], keep["mv0"][:, :, 1], ACT.Sqrt,
                                         bias=keep["eps4"][:]).then_inc(std0_done, 1)
                if on:
                    exp(2)
                    if exists(g + 1):
                        high_q(g, h + 1 if not isinstance(g, int) else (h + 1) % NH, par)
                    high(g, 7, par, 1, 0, par)
                    high(g, 8, par, 1, 1, par)
                    exp(3)

            steps(act, body)

        @block.vector
        def _(dve):
            v = nc.vector

            def low(g, k, par, u, part, p):
                dve.wait_ge(high_out, event(g, k))
                at = (slice(None), slice(4 * part, 4 * part + 4), slice(u * P, (u + 1) * P))
                v.tensor_tensor(PTL[p][at], X[:, bank(g, k, par), :].rearrange("p (k c) -> p k c", k=4), f32(PTH[p][at]),
                                ALU.subtract).then_inc(low_out, 1)

            def low_q(g, h, par):
                dve.wait_ge(high_out, event(g, 6))
                v.scalar_tensor_tensor(out=qeL[1 - par][:], in0=X[:, bank(g, 6, par), :], scalar=keep["beff"][:, ds(h, 1)],
                                       in1=f32(qeH[1 - par][:]), op0=ALU.add, op1=ALU.subtract).then_inc(low_out, 1)

            low_q(-1, 0, 1)

            def body(g, b, h, par):
                on, one, two = exists(g), exists(g - 1), exists(g - 2)

                def maximum(u):
                    col = par * UN + u
                    dve.wait_ge(scores_ready, 4 * g + u + 1)
                    v.reduce_max(mx[:, col:col + 1], S[:, u % 2, :], AX.X).then_inc(max_ready, 1)

                def negated(u):
                    col = par * UN + u
                    bias = keep["c_all"][:, ds((b * NH + h) * UN + u, 1)]
                    dve.wait_ge(max_ready, 4 * g + u + 1)
                    v.scalar_tensor_tensor(out=shift[:, col:col + 1], in0=mx[:, col:col + 1], scalar=bias, in1=bias,
                                           op0=ALU.add, op1=ALU.subtract, reverse1=True).then_inc(shift_ready, 1)

                for u in range(2):
                    if u == 1 and two:
                        dve.wait_ge(pv_done, g - 1)
                        dve.wait_ge(row_in[par], 16 * turns(g - 2, par))
                        if not isinstance(g, int) or g >= 3:
                            dve.wait_ge(wv_done, g - 2)
                        v.tensor_tensor(onorm[:], O[:], recip_row[par][:], ALU.mult).then_inc(onorm_ready, 1)
                    if on:
                        maximum(u)
                    if one:
                        low(g, 2 * u, par, 2 + u, 0, 1 - par)
                    if on:
                        negated(u)
                    if one:
                        low(g, 2 * u + 1, par, 2 + u, 1, 1 - par)
                    if u == 0 and one:
                        dve.wait_ge(probs_ready, 4 * g)
                        if not isinstance(g, int) or g >= 3:
                            dve.wait_ge(recip_out, 16 * (g - 2))
                        v.reciprocal(recip[:, (1 - par) * UN:(2 - par) * UN],
                                     rs[:, (1 - par) * UN:(2 - par) * UN]).then_inc(recip_ready, 1)
                if isinstance(g, int) and g == NG:
                    dve.wait_ge(bo_added, 1)
                    for t in range(UN):
                        dve.wait_ge(projected0, t + 1)
                        v.tensor_tensor(keep["x0"][:, t, :], projection[t], keep["x0"][:, t, :], ALU.add).then_inc(summed0, 1)
                if isinstance(g, int) and g == NG + 1:
                    dve.wait_ge(summed0, UN)
                    for t in range(UN):
                        v.bn_stats(keep["st0"][:, t, :], keep["x0"][:, t, :]).then_inc(stats0, 1)
                    dve.wait_ge(stats0, UN)
                    for t in range(UN):
                        v.bn_aggr(keep["mv0"][:, t, :], keep["st0"][:, t, :]).then_inc(stats0, 1)
                for u in (2, 3):
                    k = 4 if u == 2 else 7
                    if u == 3 and exists(g + 1) and on:
                        low_q(g, h + 1 if not isinstance(g, int) else (h + 1) % NH, par)
                    if u == 3 and isinstance(h, int) and h == 1 and b:
                        dve.wait_ge(wv_done, b * NH)
                        v.tensor_copy(keep["vsum"][:, (b - 1) * BLK:b * BLK], V[:]).then_inc(vsum_out, 1)
                    if on:
                        maximum(u)
                        low(g, k, par, u - 2, 0, par)
                        negated(u)
                        low(g, k + 1, par, u - 2, 1, par)
                if isinstance(g, int) and g == NG + 1:
                    dve.wait_ge(std0_done, 1)
                    v.reciprocal(keep["rstd0"][:], keep["std0"][:])

            steps(dve, body)


def feed_forward(nc, dram, keep):
    with ExitStack() as ctx:
        sb = lambda n, s, d=F32: ctx.enter_context(nc.sbuf_tensor(n, s, d))
        ps = lambda n: ctx.enter_context(nc.psum_tensor(n, [P, 512], F32))
        sem = lambda n: ctx.enter_context(nc.semaphore(n))
        x0, flags, wo, bo, sc, row2, eps = (keep[n] for n in ("x0", "flags", "wo", "bo", "sc", "row2", "eps4"))
        w = [keep["w0"], sb("ffn_w1", [P, KT, HID], F32R), sb("ffn_w2", [P, KT, HID], F32R)]
        sc2, spare = sb("sc2", [P, 3]), sb("spare", [P, 1])
        vs = sb("vs", [P, BLK])
        x1 = sb("x1", [P, TT, HID])
        xn2, y = sb("xn2", [P, UN, HID]), sb("y", [P, UN, HID])
        st, mv, std, rstd = sb("st4", [P, UN, 6]), sb("mv4", [P, UN, 2]), sb("std4", [P, UN]), sb("rstd4", [P, UN])
        aH = [sb(f"aH{i}", [P, KT, BLK], F32R) for i in range(3)]
        aL = [sb(f"aL{i}", [P, KT, BLK], F32R) for i in range(3)]
        hf = [sb(f"hf{i}", [P, BLK]) for i in range(2)]
        L = [ps(f"L{i}") for i in range(4)]
        C = [ps(f"C{i}") for i in range(4)]
        x_in = [sem(f"x1_in{n}") for n in range(NB)]
        names = ("vs_ready", "projected", "turned", "layers_done", "const4", "w_ready",
                 "x_bo", "summed", "stats", "std4_done", "rstd4_done", "normed", "high_in", "split_in", "relu_done",
                 "split_h", "y_done", "stored", "x0_moved")
        (vs_ready, projected, turned, layers_done, const, w_ready, x_bo, summed, stats, std_done,
         rstd_done, normed, high_in, split_in, relu_done, split_h, y_done, stored, x0_moved) = (sem(n) for n in names)
        ident = keep["ident"]
        block = ctx.enter_context(nc.Block())

        def turns(eng, head, tail):
            head(0)
            with eng.Fori(0, NB - 1) as n:
                tail(n, n + 1)
            tail(NB - 1, None)

        @block.sync
        def _(sp):
            for n in range(1, NB):
                sp.dma_start(x1[:, UN * n:UN * (n + 1), :],
                             dram["x"][n * BLK:(n + 1) * BLK, :].rearrange("(t p) d -> p t d", p=P)).then_inc(x_in[n], 16)
            with sp.Fori(0, NB - 1) as n:
                sp.wait_ge(y_done, UN * n + 2 * UN)
                sp.dma_start(dram["out"][ds(n * BLK, BLK), :].rearrange("(t p) d -> p t d", p=P), y[:]).then_inc(stored, 16)
            for t in range(UN):
                sp.wait_ge(y_done, UN * NB + t + 1)
                sp.dma_start(dram["out"][(UN * (NB - 1) + t) * P:(UN * (NB - 1) + t + 1) * P, :], y[:, t, :]).then_inc(stored, 16)
            sp.wait_ge(stored, 16 * (NB - 1 + UN) + 1)

        @block.gpsimd
        def _(pool):
            pool.sem_inc(stored, 1)
            pool.sem_inc(y_done, UN)
            for ready, count in ((vs_ready, 1), (projected, UN), (summed, UN), (stats, 2 * UN), (std_done, 1), (rstd_done, 1)):
                pool.sem_inc(ready, count)
            for n in range(1, NB):
                if n < 3:
                    for k in range(KT):
                        last = nc.gpsimd.tensor_scalar(w[n][:, k, :], flags[:, n, k, :], row2[:, k, 0:1], row2[:, k, 1:2],
                                                       ALU.mult, ALU.add)
                    last.then_inc(w_ready, 1)
                pool.wait_ge(x_in[n], 16)
                for t in range(UN * n, UN * (n + 1)):
                    last = nc.gpsimd.tensor_tensor(x1[:, t, :], x1[:, t, :], bo[:], ALU.add)
                last.then_inc(x_bo, 1)

        @block.tensor
        def _(pe):
            mm = nc.tensor.matmul

            def project(n):
                pe.wait_ge(vs_ready, n + 1)
                for t in range(UN):
                    mm(C[t][:], vs[:, t * P:(t + 1) * P], wo[:], start=True, stop=True).then_inc(projected, 1)

            def turn(n):
                pe.wait_ge(normed, UN * n + UN)
                for k in range(KT):
                    for t in range(UN):
                        last = nc.tensor.transpose(C[k][:, t * P:(t + 1) * P], xn2[:, t, k * P:(k + 1) * P], ident[:])
                    last.then_inc(turned, 1)

            def hidden(layer, ready, base, free=None):
                for m in range(KT):
                    cols = slice(m * P, (m + 1) * P)
                    if free is not None:
                        pe.wait_ge(y_done, free + m)
                    for k in range(KT):
                        if m == 0:
                            pe.wait_ge(ready, base + k + 1)
                        mm(L[m][:], w[layer][:, k, cols], aH[layer][:, k, :], start=(k == 0), stop=False)
                        last = mm(L[m][:], w[layer][:, k, cols], aL[layer][:, k, :], start=False, stop=(k == KT - 1))
                    last.then_inc(layers_done, 1)

            head = turn

            def tail(n, nxt):
                hidden(0, split_in, KT * n, free=UN * n + 1)
                if nxt is not None:
                    project(nxt)
                pe.wait_ge(w_ready, 1)
                hidden(1, split_h, 2 * KT * n)
                if nxt is not None:
                    turn(nxt)
                pe.wait_ge(w_ready, 2)
                for t in range(UN):
                    tok = slice(t * P, (t + 1) * P)
                    for k in range(KT):
                        if t == 0:
                            pe.wait_ge(split_h, 2 * KT * n + KT + k + 1)
                        mm(L[t][:], aH[2][:, k, tok], w[2][:, k, :], start=(k == 0), stop=False)
                        last = mm(L[t][:], aL[2][:, k, tok], w[2][:, k, :], start=False, stop=(k == KT - 1))
                    last.then_inc(layers_done, 1)

            turns(pe, head, tail)

        @block.scalar
        def _(act):
            def copy_sum(n):
                nc.scalar.activation(vs[:], keep["vsum"][:, ds(n * BLK, BLK)], ACT.Copy).then_inc(vs_ready, 1)

            def deviation(n):
                act.wait_ge(stats, 2 * UN * n + 2 * UN)
                nc.scalar.activation(std[:], mv[:, :, 1], ACT.Sqrt, bias=eps[:]).then_inc(std_done, 1)

            def high(n):
                for k in range(KT):
                    act.wait_ge(turned, KT * n + k + 1)
                    nc.scalar.activation(aH[0][:, k, :], C[k][:], ACT.Copy).then_inc(high_in, 1)

            def relu(n, layer):
                for m in range(KT):
                    i = layer * KT + m
                    act.wait_ge(layers_done, 3 * KT * n + i + 1)
                    if i >= 2:
                        act.wait_ge(split_h, 2 * KT * n + i - 1)
                    nc.scalar.activation(hf[m % 2][:], L[m][:], ACT.Relu, scale=sc2[:, layer:layer + 1])
                    nc.scalar.activation(aH[layer + 1][:, m, :], L[m][:], ACT.Relu,
                                         scale=sc2[:, layer:layer + 1]).then_inc(relu_done, 1)

            def head(n):
                nc.scalar.activation(x1[:, 0:UN, :], x0[:], ACT.Copy).then_inc(x0_moved, 1)
                high(n)
                act.wait_ge(const, 1)

            def tail(n, nxt):
                if nxt is not None:
                    act.wait_ge(projected, UN * nxt)
                    copy_sum(nxt)
                relu(n, 0)
                if nxt is not None:
                    deviation(nxt)
                relu(n, 1)
                if nxt is not None:
                    high(nxt)

            turns(act, head, tail)

        @block.vector
        def _(dve):
            v = nc.vector
            v.tensor_scalar(sc2[:], sc[:], 2.0, None, ALU.mult).then_inc(const, 1)

            def norm(n):
                dve.wait_ge(x_bo, n)
                for t in range(UN):
                    row_t = x1[:, ds(UN * n + t, 1), :].rearrange("p o d -> p (o d)")
                    dve.wait_ge(projected, UN * n + t + 1)
                    v.tensor_tensor(row_t, C[t][:], row_t, ALU.add).then_inc(summed, 1)
                dve.wait_ge(summed, UN * n + UN)
                v.memset(spare[:], 0.0)
                for t in range(UN):
                    v.bn_stats(st[:, t, :], x1[:, ds(UN * n + t, 1), :].rearrange("p o d -> p (o d)")).then_inc(stats, 1)
                dve.wait_ge(stats, 2 * UN * n + UN)
                v.memset(spare[:], 0.0)
                for t in range(UN):
                    v.bn_aggr(mv[:, t, :], st[:, t, :]).then_inc(stats, 1)
                dve.wait_ge(std_done, n + 1)
                v.reciprocal(rstd[:], std[:]).then_inc(rstd_done, 1)
                dve.wait_ge(rstd_done, n + 1)
                for t in range(UN):
                    v.tensor_scalar(xn2[:, t, :], x1[:, ds(UN * n + t, 1), :].rearrange("p o d -> p (o d)"),
                                    mv[:, t, 0:1], rstd[:, t:t + 1], ALU.subtract, ALU.mult).then_inc(normed, 1)

            def low(n):
                for k in range(KT):
                    dve.wait_ge(high_in, KT * n + k + 1)
                    v.tensor_tensor(aL[0][:, k, :], C[k][:], f32(aH[0][:, k, :]), ALU.subtract).then_inc(split_in, 1)

            def split(n, layer):
                for m in range(KT):
                    dve.wait_ge(relu_done, 2 * KT * n + layer * KT + m + 1)
                    v.tensor_tensor(aL[layer + 1][:, m, :], hf[m % 2][:], f32(aH[layer + 1][:, m, :]),
                                    ALU.subtract).then_inc(split_h, 1)

            def head(n):
                for t in range(UN):
                    v.tensor_scalar(xn2[:, t, :], x0[:, t, :], keep["mv0"][:, t, 0:1], keep["rstd0"][:, t:t + 1],
                                    ALU.subtract, ALU.mult).then_inc(normed, 1)
                low(n)
                dve.wait_ge(x0_moved, 1)

            def tail(n, nxt):
                split(n, 0)
                if nxt is not None:
                    norm(nxt)
                split(n, 1)
                if nxt is not None:
                    low(nxt)
                dve.wait_ge(stored, 16 * n + 1)
                for t in range(UN):
                    dve.wait_ge(layers_done, 3 * KT * n + 2 * KT + t + 1)
                    v.scalar_tensor_tensor(out=y[:, t, :], in0=L[t][:], scalar=sc[:, 2:3],
                                           in1=x1[:, ds(UN * n + t, 1), :].rearrange("p o d -> p (o d)"),
                                           op0=ALU.mult, op1=ALU.add).then_inc(y_done, 1)

            turns(dve, head, tail)


def layer(nc, dram):
    with ExitStack() as ctx:
        sb = lambda c, n, s, d=F32: c.enter_context(nc.sbuf_tensor(n, s, d))
        keep = {"ident": sb(ctx, "ident", [P, P]), "vsum": sb(ctx, "vsum", [P, TOK])}
        keep |= {
            "x0": sb(ctx, "x0", [P, UN, HID]), "wo": sb(ctx, "wo", [P, HID]), "bo": sb(ctx, "bo", [P, HID]),
            "flags": sb(ctx, "flags", [P, 3, KT, HID], U8), "sc": sb(ctx, "sc", [P, 3]),
            "w0": sb(ctx, "ffn_w0", [P, KT, HID], F32R), "row": sb(ctx, "row", [P, KT]),
            "row2": sb(ctx, "row2", [P, KT, 2]), "eps4": sb(ctx, "eps4", [P, 1]),
            "st0": sb(ctx, "st0", [P, UN, 6]), "mv0": sb(ctx, "mv0", [P, UN, 2]),
            "std0": sb(ctx, "std0", [P, UN]), "rstd0": sb(ctx, "rstd0", [P, UN]),
        }
        with ExitStack() as inner:
            keep |= {
                "weff": [sb(inner, f"weff{i}", [P, 3, P], F32R) for i in range(2)],
                "weff_in": [inner.enter_context(nc.semaphore(f"weff_in{i}")) for i in range(2)],
                "beff": sb(inner, "beff", [P, NH]), "c_all": sb(inner, "c_all", [P, NG * UN]),
                "kvTH": sb(inner, "kvTH", [P, TOK], F32R), "kvTL": sb(inner, "kvTL", [P, TOK], F32R),
                "kvn": sb(inner, "kvn", [P, TT, P], F32R),
                "qaH": sb(inner, "qaH", [P, TOK], F32R), "qaL": sb(inner, "qaL", [P, TOK], F32R),
                "qbH": sb(inner, "qbH", [P, TOK], F32R), "qbL": sb(inner, "qbL", [P, TOK], F32R),
            }
            prepare(nc, dram, keep)
            attention(nc, dram, keep)
        feed_forward(nc, dram, keep)


def laid_out(a):
    t = lambda n: np.asarray(a["L0_attn_" + n])
    wq = t("Wq_up").reshape(NH, QHEAD, QL)
    bq = t("bq_up").reshape(NH, QHEAD)
    wkv = t("Wkv_up").reshape(NH, NOPE + VH, KVL)
    bkv = t("bkv_up").reshape(NH, NOPE + VH)
    twice = np.r_[0:P, P:QL, P:QL]
    raw = np.concatenate([wq[:, :NOPE], wkv[:, :NOPE], bkv[:, :NOPE, None], bq[:, :NOPE, None],
                          wq[:, NOPE:].transpose(0, 2, 1)[:, 0:P],
                          wq[:, NOPE:].transpose(0, 2, 1)[:, np.r_[P:QL, P:QL]]], axis=2)
    wvT = wkv[:, NOPE:].transpose(0, 2, 1)
    bqc = t("bq_c")
    out = {
        "x": t("hidden_size").reshape(TOK, HID),
        "raw": raw.reshape(NH // HG, HG, P, R_N).transpose(0, 2, 1, 3).reshape(NH // HG, P, HG * R_N),
        "bqrT": bq[:, NOPE:].T,
        "wlT": np.concatenate([t("Wkv_c").T, t("Wq_c").T[:, twice]], axis=1),
        "pb": np.stack([t("bkv_c"), bqc[:P], bqc[np.r_[P:QL, P:QL]]], axis=1),
        "wv": np.concatenate([wvT, wvT], axis=1), "bv": bkv[:, NOPE:],
        "woT": t("Wo").T, "bo": t("bo"),
    }
    for j in range(3):
        out[f"k{j}"] = np.asarray(a[f"L0_ffn_k{j}"])
        out[f"s{j}"] = np.asarray(a[f"L0_ffn_s{j}"]).reshape(1)
    return {n: np.ascontiguousarray(v) for n, v in out.items()}


def kernel(**inputs):
    import concourse.bacc as bacc
    from concourse.bass_utils import run_bass_kernel_spmd

    nc = bacc.Bacc("TRN2", target_bir_lowering=False, num_devices=1)
    arrays = laid_out(inputs)
    dram = {n: nc.dram_tensor("in_" + n, v.shape, mybir.dt.from_np(v.dtype), kind="ExternalInput").ap()
            for n, v in arrays.items()}
    dram["out"] = nc.dram_tensor("out", (TOK, HID), F32, kind="ExternalOutput").ap()
    dram["weff"] = nc.dram_tensor("weff_scratch", (NH // HG, HG, P, 3 * P), F32, kind="Internal").ap()
    dram["weff_h"] = dram["weff"].rearrange("g h p c -> (g h) p c")
    dram["row"] = nc.dram_tensor("row_scratch", (2, BLK), F32, kind="Internal").ap()
    layer(nc, dram)
    r = run_bass_kernel_spmd(nc, [{"in_" + n: v for n, v in arrays.items()}], core_ids=[0])
    return r.results[0]["out"].reshape(BATCH, SEQ, HID)
```
